# Optimizing a Trainium2 kernel written in Bass

```python
import numpy as np
import jax
import jax.numpy as jnp

def _softmax(x, axis=-1):
    return jax.nn.softmax(x, axis=axis)

def _gelu(x):
    return jax.nn.gelu(x, approximate=True)

def _silu(x):
    return jax.nn.silu(x)

def _sigmoid(x):
    return jax.nn.sigmoid(x)

def _layernorm(x, axis=-1, eps=1e-05):
    m = jnp.mean(x, axis=axis, keepdims=True)
    v = jnp.var(x, axis=axis, keepdims=True)
    return (x - m) / jnp.sqrt(v + eps)

def _scatter_add(tgt, idx, src, axis=0):
    return tgt.at[idx].add(src)

def _segment_sum(src, seg, n):
    return jax.ops.segment_sum(src, seg, n)
kernel_name = 'mk_flamingo_gated_d1_seqx_r8_60bf08'

def setup_inputs(seed: int=0):
    np.random.seed(seed)
    _w = jnp.asarray

    def _rec_inputs():
        import jax
        import jax.numpy as jnp
        _rk = jax.random.key(seed)
        x = 7.22e-05 + 1 * jax.random.normal(jax.random.fold_in(_rk, 1), (8, 128, 512), jnp.float32)
        _lenS = 128 - jax.random.randint(jax.random.fold_in(_rk, 7), (8,), 0, max(1, 128 // 4) + 1, jnp.int32)
        _lenS2 = 128 - jax.random.randint(jax.random.fold_in(_rk, 8), (8,), 0, max(1, 128 // 4) + 1, jnp.int32)
        _ctx_4096P = jax.random.normal(jax.random.fold_in(_rk, 11), (8, 16, 512), jnp.float32)
        _ctx_4096c = jax.random.dirichlet(jax.random.fold_in(_rk, 511), 0.3 * jnp.ones((16,), jnp.float32), (8, 128))
        _ctx_4096t = jnp.einsum('bsk,bkd->bsd', _ctx_4096c, _ctx_4096P)
        _ctx_4096t = _ctx_4096t * jax.lax.rsqrt(jnp.mean(jnp.square(_ctx_4096t)) + 1e-12) * 0.953939
        ctx_4096 = 4.13588e-05 + 0.999923 * (_ctx_4096t + 0.3 * jax.random.normal(jax.random.fold_in(_rk, 611), (8, 128, 512), jnp.float32))
        _g = jax.random.normal(jax.random.fold_in(_rk, 9001), (2, 1), jnp.float32)
        _g = jnp.sign(_g) * jnp.maximum(jnp.abs(_g), 1.0) + (_g == 0) * 1.0
        g_xattn = _g[0]
        g_ffn = _g[1]
        return (x, ctx_4096, g_xattn, g_ffn)
    x, ctx_4096, g_xattn, g_ffn = _rec_inputs()

    def _L0_xattn_setup():
        import jax, jax.numpy as jnp
        import numpy as np
        B, S, D = (1, 256, 512)
        H, HKV, DK, DV = (32, 8, 128, 128)
        key = jax.random.key(seed)
        ks = jax.random.split(key, 7)
        std = 0.02
        return {'q': jax.random.normal(ks[0], (B, S, D), jnp.float32), 'k': jax.random.normal(ks[1], (B, S, D), jnp.float32), 'v': jax.random.normal(ks[2], (B, S, D), jnp.float32), 'Wq': jax.random.normal(ks[3], (H * DK, D), jnp.float32) * std, 'Wk': jax.random.normal(ks[4], (HKV * DK, D), jnp.float32) * std, 'Wv': jax.random.normal(ks[5], (HKV * DV, D), jnp.float32) * std, 'Wd': jax.random.normal(ks[6], (D, H * DV), jnp.float32) * std}
    _L0_xattn_all = _L0_xattn_setup()
    _L0_xattn_in = {k: v for k, v in _L0_xattn_all.items() if k in ('Wq', 'Wk', 'Wv', 'Wd')}
    del _L0_xattn_all

    def _L0_ffn_setup():
        import jax, jax.numpy as jnp
        import numpy as np
        BLOCK = 64
        NF4_CODE = jnp.array([-1.0, -0.6961928009986877, -0.5250730514526367, -0.39491748809814453, -0.28444138169288635, -0.18477343022823334, -0.09105003625154495, 0.0, 0.07958029955625534, 0.16093020141124725, 0.24611230194568634, 0.33791524171829224, 0.44070982933044434, 0.5626170039176941, 0.7229568362236023, 1.0], dtype=jnp.float32)

        def dequant_nf4(q, absmax, shape):
            w = NF4_CODE[q.reshape(-1)]
            w = w.reshape(-1, BLOCK) * absmax[:, None]
            return w.reshape(shape)
        key = jax.random.key(seed)
        ks = jax.random.split(key, 7)
        HD, M = (512, 1792)
        nblk = HD * M // BLOCK
        x = jax.random.normal(ks[0], (2, 256, HD), dtype=jnp.float32)
        gate_q = jax.random.randint(ks[1], (M, HD), 0, 16, dtype=jnp.int32)
        up_q = jax.random.randint(ks[2], (M, HD), 0, 16, dtype=jnp.int32)
        down_q = jax.random.randint(ks[3], (HD, M), 0, 16, dtype=jnp.int32)
        gate_absmax = jax.random.uniform(ks[4], (nblk,), dtype=jnp.float32) * 0.05
        up_absmax = jax.random.uniform(ks[5], (nblk,), dtype=jnp.float32) * 0.05
        down_absmax = jax.random.uniform(ks[6], (nblk,), dtype=jnp.float32) * 0.05
        return {'x': x, 'gate_q': gate_q, 'gate_absmax': gate_absmax, 'up_q': up_q, 'up_absmax': up_absmax, 'down_q': down_q, 'down_absmax': down_absmax}
    _L0_ffn_all = _L0_ffn_setup()
    _L0_ffn_in = {k: v for k, v in _L0_ffn_all.items() if k in ('gate_q', 'gate_absmax', 'up_q', 'up_absmax', 'down_q', 'down_absmax')}
    del _L0_ffn_all
    return {'x': x, 'ctx_4096': ctx_4096, 'g_xattn': g_xattn, 'g_ffn': g_ffn, 'L0_xattn_Wq': _L0_xattn_in['Wq'], 'L0_xattn_Wk': _L0_xattn_in['Wk'], 'L0_xattn_Wv': _L0_xattn_in['Wv'], 'L0_xattn_Wd': _L0_xattn_in['Wd'], 'L0_ffn_gate_q': _L0_ffn_in['gate_q'], 'L0_ffn_gate_absmax': _L0_ffn_in['gate_absmax'], 'L0_ffn_up_q': _L0_ffn_in['up_q'], 'L0_ffn_up_absmax': _L0_ffn_in['up_absmax'], 'L0_ffn_down_q': _L0_ffn_in['down_q'], 'L0_ffn_down_absmax': _L0_ffn_in['down_absmax']}

def reference(x, ctx_4096, g_xattn, g_ffn, L0_xattn_Wq, L0_xattn_Wk, L0_xattn_Wv, L0_xattn_Wd, L0_ffn_gate_q, L0_ffn_gate_absmax, L0_ffn_up_q, L0_ffn_up_absmax, L0_ffn_down_q, L0_ffn_down_absmax):
    import jax
    import jax.numpy as jnp

    def _L0_xattn_ref(q, k, v, Wq, Wk, Wv, Wd):
        import jax, jax.numpy as jnp
        import numpy as np
        B, S, D = (1, 256, 512)
        H, HKV, DK, DV = (32, 8, 128, 128)
        b, s, _ = q.shape
        exp = H // HKV
        Q = (q @ Wq.T).reshape(b, s, HKV, exp, DK)
        K = (k @ Wk.T).reshape(b, s, HKV, DK)
        V = (v @ Wv.T).reshape(b, s, HKV, DV)
        scale = DK ** (-0.5)
        scores = jnp.einsum('bqhed,bkhd->bheqk', Q, K) * scale
        causal = jnp.tril(jnp.ones((s, s), dtype=bool))
        scores = jnp.where(causal, scores, jnp.finfo(scores.dtype).min)
        probs = jax.nn.softmax(scores, axis=-1)
        attn = jnp.einsum('bheqk,bkhd->bqhed', probs, V)
        attn = attn.reshape(b, s, H * DV)
        return attn @ Wd.T

    def _L0_ffn_ref(x, gate_q, gate_absmax, up_q, up_absmax, down_q, down_absmax):
        import jax, jax.numpy as jnp
        import numpy as np
        BLOCK = 64
        NF4_CODE = jnp.array([-1.0, -0.6961928009986877, -0.5250730514526367, -0.39491748809814453, -0.28444138169288635, -0.18477343022823334, -0.09105003625154495, 0.0, 0.07958029955625534, 0.16093020141124725, 0.24611230194568634, 0.33791524171829224, 0.44070982933044434, 0.5626170039176941, 0.7229568362236023, 1.0], dtype=jnp.float32)

        def dequant_nf4(q, absmax, shape):
            w = NF4_CODE[q.reshape(-1)]
            w = w.reshape(-1, BLOCK) * absmax[:, None]
            return w.reshape(shape)
        HD = x.shape[-1]
        M = gate_q.shape[0]
        Wg = dequant_nf4(gate_q, gate_absmax, (M, HD))
        Wu = dequant_nf4(up_q, up_absmax, (M, HD))
        Wd = dequant_nf4(down_q, down_absmax, (HD, M))
        g = jnp.einsum('bsh,mh->bsm', x, Wg)
        u = jnp.einsum('bsh,mh->bsm', x, Wu)
        h = jax.nn.silu(g) * u
        return jnp.einsum('bsm,hm->bsh', h, Wd)
    x = x + jnp.tanh(g_xattn[0]) * _L0_xattn_ref(_layernorm(x, axis=-1), ctx_4096, ctx_4096, L0_xattn_Wq, L0_xattn_Wk, L0_xattn_Wv, L0_xattn_Wd)
    x = x + jnp.tanh(g_ffn[0]) * _L0_ffn_ref(_layernorm(x, axis=-1), L0_ffn_gate_q, L0_ffn_gate_absmax, L0_ffn_up_q, L0_ffn_up_absmax, L0_ffn_down_q, L0_ffn_down_absmax)
    return x

_drawn_inputs = setup_inputs


def setup_inputs(seed=0):
    import zlib

    import numpy as np

    out = dict(_drawn_inputs(seed))
    spreads = {}
    factors = {'L0_xattn_Wq': 2.952,
     'L0_xattn_Wk': 2.941,
     'L0_ffn_gate_absmax': 3.266,
     'L0_ffn_up_absmax': 3.288,
     'L0_ffn_down_absmax': 3.299}
    for name, (base, spread) in spreads.items():
        noise = np.random.default_rng([zlib.crc32(name.encode()), seed]).standard_normal(out[name].shape)
        drawn = base * np.exp(spread * noise) if base else spread * noise
        out[name] = jnp.asarray(drawn.astype(out[name].dtype))
    for name, factor in factors.items():
        out[name] = (out[name] * factor).astype(out[name].dtype)
    return out
```

```python
from contextlib import ExitStack

import concourse.bass as bass
from concourse import mybir

ALU = mybir.AluOpType
ACT = mybir.ActivationFunctionType
F32 = mybir.dt.float32
F32R = mybir.dt.float32r
I32 = mybir.dt.int32
AX_X = mybir.AxisListType.X

P = 128
B, S, D = 8, 128, 512
TOK = B * S
HALF = TOK // 2
KT = D // P
NG, NE = 8, 4
M = 1792
MT = M // P
SCALE = float(P) ** -0.5
EPS = 1e-5
MASKED = -3.0e38

W_KV = 2 * KT * P
W_Q = KT * NE * P
W_D = NE * D
W_G = W_KV + W_Q + W_D
PIECE_A = (W_KV + W_Q) // 2
PIECE_B = W_D // 2

FF_J = 3 * D
FF = MT * FF_J
CHUNKS = NG * B
CH = FF // CHUNKS

PROJ = 12
Q_ONLY = 4
LN_T = 8

LINE = {
    (8, 9): (0.08134990185499191, -0.001769605907611549),
    (10, 11): (0.0918029248714447, -0.029296472668647766),
    (12, 13): (0.12190712988376617, -0.16882582008838654),
    (14, 15): (0.2770431637763977, -1.2163453102111816),
    (0, 1): (0.30380716919898987, 1.1266502141952515),
    (2, 3): (0.1301555335521698, 0.12570463120937347),
    (4, 5): (0.09966793656349182, 0.014562436379492283),
    (6, 7): (0.09105003625154495, 0.0),
}
ACT_LINES = ((8, 9), (14, 15), (0, 1), (10, 11))
POOL_LINES = ((2, 3), (4, 5), (12, 13))


def steps(last):
    at = [("K", 0), ("K", 1), ("V", 2), ("S", 0), ("V", 3), ("S", 1), ("T", 0), ("S", 2),
          ("O", 0), ("T", 1), ("Y", 0), ("S", 3), ("O", 1), ("T", 2), ("Y", 1), ("Q", 4), ("Q", 5),
          ("O", 2), ("T", 3), ("Y", 2), ("Q", 6), ("Q", 7), ("O", 3), ("Y", 3), ("S", 4), ("S", 5),
          ("T", 4), ("S", 6), ("O", 4), ("T", 5), ("Y", 4), ("S", 7), ("O", 5), ("T", 6), ("Y", 5),
          ("O", 6), ("T", 7), ("Y", 6)]
    following = [] if last else [("Q", n) for n in range(8, PROJ)]
    return at + following[:1] + [("O", 7)] + following[1:] + [("Y", 7)]


def wait_past(engine, semaphore, count):
    if not isinstance(count, int) or count > 0:
        engine.wait_ge(semaphore, count)


def flamingo(nc, x, ctx_t, gates, w_groups, ff_q, ff_absmax, out):
    ff_w = nc.dram_tensor("ff_dequantised", (P, FF), F32, kind="Internal").ap()
    with ExitStack() as stack:
        def sb(name, shape, dt=F32, on=None):
            return (on or stack).enter_context(nc.sbuf_tensor(name, shape, dt))

        def sem(name):
            return stack.enter_context(nc.semaphore(name))

        banks = [stack.enter_context(nc.psum_tensor(f"bank{i}", [P, D], F32)) for i in range(8)]
        proj_ps, s_ps, t_ps, o_ps, y_ps = banks[0:2], banks[2:4], banks[4], banks[5], banks[6:8]

        xs = sb("xs", [P, B, D])
        ln_hi = sb("ln_hi", [P, KT, TOK], F32R)
        ln_lo = sb("ln_lo", [P, KT, TOK], F32R)
        ident = sb("ident", [P, P])
        mask = sb("mask", [P, P])
        gate_raw = sb("gate_raw", [P, 2])
        gate = sb("gate", [P, 2])
        stats = sb("stats", [P, B, 6])
        mv = sb("mv", [P, B, 2])
        rstd = sb("rstd", [P, B])
        eps_var = sb("eps_var", [P, B])
        minus_half = sb("minus_half", [P, B])
        line_at = sb("line_at", [P, 16])

        attn = ExitStack()
        ctx_hi = sb("ctx_hi", [P, KT, TOK], F32R, attn)
        ctx_lo = sb("ctx_lo", [P, KT, TOK], F32R, attn)
        w_raw_a = sb("w_raw_a", [P, PIECE_A], F32, attn)
        w_raw_b = sb("w_raw_b", [P, PIECE_B], F32, attn)
        w_hi = sb("w_hi", [P, W_G], F32R, attn)
        w_lo = sb("w_lo", [P, W_G], F32R, attn)
        k_hi = sb("k_hi", [P, TOK], F32R, attn)
        k_lo = sb("k_lo", [P, TOK], F32R, attn)
        v_hi = sb("v_hi", [P, B, P], F32R, attn)
        v_lo = sb("v_lo", [P, B, P], F32R, attn)
        q_hi = sb("q_hi", [P, NE, HALF], F32R, attn)
        q_lo = sb("q_lo", [P, NE, HALF], F32R, attn)
        prob = [sb(f"prob{i}", [P, NE, P], F32, attn) for i in range(2)]
        bias = [sb(f"bias{i}", [P, NE], F32, attn) for i in range(2)]
        rsum = [sb(f"rsum{i}", [P, NE], F32, attn) for i in range(2)]
        rinv = [sb(f"rinv{i}", [P, NE], F32, attn) for i in range(2)]
        q_raw = sb("q_raw", [P, CH], I32, attn)
        absmax = sb("absmax", [P, CH], F32, attn)
        q_c = [sb(f"q_c{i}", [P, CH], F32, attn) for i in range(2)]
        line = [{k: sb(f"line{k[0]}_{i}", [P, CH], F32, attn) for k in LINE if k != (6, 7)} for i in range(2)]
        w_out = sb("w_out", [P, CH], F32, attn)
        with ExitStack() as first:
            ctx_raw = sb("ctx_raw", [P, KT, TOK], F32, first)
        pt_hi = [sb(f"pt_hi{i}", [P, NE, P], F32R, attn) for i in range(2)]
        pt_lo = [sb(f"pt_lo{i}", [P, NE, P], F32R, attn) for i in range(2)]
        ot_hi = [sb(f"ot_hi{i}", [P, NE, P], F32R, attn) for i in range(2)]
        ot_lo = [sb(f"ot_lo{i}", [P, NE, P], F32R, attn) for i in range(2)]
        attn.close()

        ffs = ExitStack()
        h = sb("h", [P, MT, TOK], F32, ffs)
        gu_raw = [sb(f"gu_raw{i}", [P, 2 * D], F32, ffs) for i in range(2)]
        gu_hi = [sb(f"gu_hi{i}", [P, 2, KT, P], F32R, ffs) for i in range(2)]
        gu_lo = [sb(f"gu_lo{i}", [P, 2, KT, P], F32R, ffs) for i in range(2)]
        silu = [sb(f"silu{i}", [P, HALF], F32, ffs) for i in range(2)]
        dn_raw = [sb(f"dn_raw{i}", [P, D], F32, ffs) for i in range(2)]
        dn_hi = [sb(f"dn_hi{i}", [P, D], F32R, ffs) for i in range(2)]
        dn_lo = [sb(f"dn_lo{i}", [P, D], F32R, ffs) for i in range(2)]
        h_hi = [sb(f"h_hi{i}", [P, TOK], F32R, ffs) for i in range(2)]
        h_lo = [sb(f"h_lo{i}", [P, TOK], F32R, ffs) for i in range(2)]
        xn = [sb(f"xn{i}", [P, D], F32, ffs) for i in range(2)]
        ffs.close()

        x_in, ctx_in, gates_in = sem("x_in"), sem("ctx_in"), sem("gates_in")
        wa_in, wb_in = sem("wa_in"), sem("wb_in")
        q_in, absmax_in, w_stored = sem("q_in"), sem("absmax_in"), sem("w_stored")
        gu_in = [sem(f"gu_in{i}") for i in range(2)]
        dn_in = [sem(f"dn_in{i}") for i in range(2)]
        out_done = sem("out_done")
        ident_zero, ident_done, mask_zero, mask_done = sem("ident_zero"), sem("ident_done"), sem("mask_zero"), sem("mask_done")
        half_set, line_at_set, gate_done = sem("half_set"), sem("line_at_set"), sem("gate_done")
        stats_done, mv_done, eps_done, rstd_done = sem("stats_done"), sem("mv_done"), sem("eps_done"), sem("rstd_done")
        xn_done, ln_turned, ln_hi_done, ln_split = sem("xn_done"), sem("ln_turned"), sem("ln_hi_done"), sem("ln_split")
        ctx_hi_done, ctx_split = sem("ctx_hi_done"), sem("ctx_split")
        wa_hi, wa_split, wb_hi, wb_split = sem("wa_hi"), sem("wa_split"), sem("wb_hi"), sem("wb_split")
        proj_done, proj_hi, proj_split = sem("proj_done"), sem("proj_hi"), sem("proj_split")
        s_done, s_masked, max_done, bias_done = sem("s_done"), sem("s_masked"), sem("max_done"), sem("bias_done")
        exp_done, rinv_done, norm_done = sem("exp_done"), sem("rinv_done"), sem("norm_done")
        t_done, pt_hi_done, pt_split = sem("t_done"), sem("pt_hi_done"), sem("pt_split")
        o_done, ot_hi_done, ot_split = sem("o_done"), sem("ot_hi_done"), sem("ot_split")
        y_done, y_added = sem("y_done"), sem("y_added")
        qc_done, act_lines, pool_lines = sem("qc_done"), sem("act_lines"), sem("pool_lines")
        env_step, env_done, w_scaled = sem("env_step"), sem("env_done"), sem("w_scaled")
        gu_hi_done, gu_split = sem("gu_hi_done"), sem("gu_split")
        g_done, u_done, silu_done, h_done = sem("g_done"), sem("u_done"), sem("silu_done"), sem("h_done")
        dn_hi_done, dn_split, hh_done, h_split = sem("dn_hi_done"), sem("dn_split"), sem("hh_done"), sem("h_split")
        down_done, fin_ready, fin_done = sem("down_done"), sem("fin_ready"), sem("fin_done")

        def f32(ap):
            return ap.bitcast(F32)

        def flat(tile):
            return tile[:, :, :].rearrange("p a b -> p (a b)")

        def h_cols(j, t=None):
            at, n = (j * TOK, TOK) if t is None else (j * TOK + t * HALF, HALF)
            return h[:, :, :].rearrange("p j t -> p (j t)")[:, bass.ds(at, n)]

        def wk(w, kt):
            return w[:, kt * P:(kt + 1) * P]

        def wv(w, kt):
            return w[:, KT * P + kt * P:KT * P + (kt + 1) * P]

        def wq(w, kt, e):
            at = W_KV + kt * NE * P + e * P
            return w[:, at:at + P]

        def wd(w, e):
            at = W_KV + W_Q + e * D
            return w[:, at:at + D]

        def proj_dst(n, k, v, q):
            if n < 2:
                return k[:, n * HALF:(n + 1) * HALF]
            if n < 4:
                return v[:, (n - 2) * 4:(n - 1) * 4, :].rearrange("p b d -> p (b d)")
            return q[:, n % 4, :]

        def nproj(g, n):
            return g * PROJ + (Q_ONLY + n + 1)

        def ln_vector(dve, done, tmp):
            for b in range(B):
                nc.vector.bn_stats(stats[:, b, :], xs[:, b, :]).then_inc(stats_done, 1)
            for b in range(B):
                dve.wait_ge(stats_done, done + b + 1)
                nc.vector.bn_aggr(mv[:, b, :], stats[:, b, :]).then_inc(mv_done, 1)
            dve.wait_ge(mv_done, done + B)
            nc.vector.tensor_scalar(eps_var[:, :], mv[:, :, 1], EPS, None, ALU.add).then_inc(eps_done, 1)
            dve.wait_ge(rstd_done, done // B + 1)
            for b in range(B):
                if b >= 2:
                    dve.wait_ge(ln_turned, done + b - 1)
                nc.vector.tensor_scalar(tmp(b), xs[:, b, :], mv[:, b, 0:1], rstd[:, b:b + 1],
                                        ALU.subtract, ALU.mult).then_inc(xn_done, 1)
                if b >= 1:
                    ln_low(dve, done, b - 1)
            ln_low(dve, done, B - 1)

        def ln_low(dve, done, b):
            dve.wait_ge(ln_hi_done, done + b + 1)
            at = slice(b * P, (b + 1) * P)
            nc.vector.tensor_tensor(ln_lo[:, :, at], banks[b % 2][:, :].rearrange("p (k t) -> p k t", k=KT),
                                    f32(ln_hi[:, :, at]), ALU.subtract).then_inc(ln_split, 1)

        def ln_scalar(act, done):
            for b in range(B):
                act.wait_ge(ln_turned, done + b + 1)
                nc.scalar.activation(ln_hi[:, :, b * P:(b + 1) * P],
                                     banks[b % 2][:, :].rearrange("p (k t) -> p k t", k=KT),
                                     ACT.Copy).then_inc(ln_hi_done, 1)

        def ln_tensor(pe, done, tmp):
            for b in range(B):
                pe.wait_ge(xn_done, done + b + 1)
                if b >= 2:
                    pe.wait_ge(ln_split, done + b - 1)
                for k in range(KT):
                    mm = nc.tensor.transpose(banks[b % 2][:, k * P:(k + 1) * P], tmp(b)[:, k * P:(k + 1) * P], ident[:, :])
                mm.then_inc(ln_turned, 1)

        def prob_tile(b):
            return flat(prob[b % 2])

        def xn_tile(b):
            return xn[b % 2][:, :]

        block = stack.enter_context(nc.Block())

        @block.sync
        def _(sp):
            sp.dma_start(xs[:, :, :], x.rearrange("b s d -> s b d")).then_inc(x_in, 16)
            sp.dma_start(gate_raw[:, :], gates.partition_broadcast(P)).then_inc(gates_in, 16)
            sp.dma_start(ctx_raw[:, :, :], ctx_t.rearrange("(k p) t -> p k t", p=P)).then_inc(ctx_in, 16)

            def load_q(c):
                wait_past(sp, qc_done, c)
                sp.dma_start(q_raw[:, :], ff_q[:, bass.ds(c * CH, CH)]).then_inc(q_in, 16)

            def load_absmax(c):
                for i in range(2):
                    sp.dma_start(absmax[64 * i:64 * (i + 1), :],
                                 ff_absmax[i, bass.ds(c * CH, CH)].partition_broadcast(64)).then_inc(absmax_in, 16)

            def store(c):
                sp.wait_ge(w_scaled, c + 1)
                sp.dma_start(ff_w[:, bass.ds(c * CH, CH)], w_out[:, :]).then_inc(w_stored, 16)

            load_q(0)
            load_absmax(0)
            load_q(1)
            load_q(2)
            with sp.Fori(2, CHUNKS - 1) as c:
                load_q(c + 1)
                store(c - 2)
                load_absmax(c - 1)
            for c in range(CHUNKS - 3, CHUNKS):
                store(c)
                if c + 1 < CHUNKS:
                    load_absmax(c + 1)
            sp.wait_ge(w_stored, 16 * CHUNKS)
            sp.wait_ge(ln_split, 2 * B)

            def load_gu(j, i, free):
                if free:
                    sp.wait_ge(gu_split, j - 1)
                sp.dma_start(gu_raw[i][:, :], ff_w[:, bass.ds(j * FF_J, 2 * D)]).then_inc(gu_in[i], 16)

            def load_dn(j, i, free):
                if free:
                    sp.wait_ge(dn_split, j - 1)
                sp.dma_start(dn_raw[i][:, :], ff_w[:, bass.ds(j * FF_J + 2 * D, D)]).then_inc(dn_in[i], 16)

            for i in range(2):
                load_gu(i, i, False)
                load_dn(i, i, False)
            with sp.Fori(1, MT // 2) as jj:
                for i in range(2):
                    load_gu(jj * 2 + i, i, True)
            with sp.Fori(1, MT // 2) as jj:
                for i in range(2):
                    load_dn(jj * 2 + i, i, True)
            for b in range(B):
                sp.wait_ge(fin_done, b + 1)
                sp.dma_start(out[b], xs[:, b, :]).then_inc(out_done, 16)
            sp.wait_ge(out_done, 16 * B)

        @block.gpsimd
        def _(pool):
            nc.gpsimd.memset(ident[:, :], 0.0).then_inc(ident_zero, 1)
            nc.gpsimd.memset(mask[:, :], 0.0).then_inc(mask_zero, 1)
            nc.gpsimd.memset(minus_half[:, :], -0.5).then_inc(half_set, 1)

            def load_a(g, i):
                pool.dma_start(w_raw_a[:, :], w_groups[g, :, i * PIECE_A:(i + 1) * PIECE_A]).then_inc(wa_in, 16)

            def load_b(g, i):
                at = W_KV + W_Q + i * PIECE_B
                pool.dma_start(w_raw_b[:, :], w_groups[g, :, at:at + PIECE_B]).then_inc(wb_in, 16)

            load_a(0, 0)
            load_b(0, 0)
            pool.wait_ge(ident_zero, 1)
            nc.gpsimd.affine_select(out=ident[:, :], in_=ident[:, :], compare_op=ALU.not_equal, fill=1.0, base=0,
                                    pattern=[[-1, P]], channel_multiplier=1).then_inc(ident_done, 1)
            pool.wait_ge(mask_zero, 1)
            nc.gpsimd.affine_select(out=mask[:, :], in_=mask[:, :], compare_op=ALU.is_ge, fill=MASKED, base=0,
                                    pattern=[[-1, P]], channel_multiplier=1).then_inc(mask_done, 1)

            def low_a(n, i):
                pool.wait_ge(wa_hi, n + 1)
                at = slice(i * PIECE_A, (i + 1) * PIECE_A)
                nc.gpsimd.tensor_tensor(w_lo[:, at], w_raw_a[:, :], f32(w_hi[:, at]), ALU.subtract).then_inc(wa_split, 1)
                pool.wait_ge(wa_split, n + 1)

            def low_b(n, i):
                pool.wait_ge(wb_hi, n + 1)
                at = slice(W_KV + W_Q + i * PIECE_B, W_KV + W_Q + (i + 1) * PIECE_B)
                nc.gpsimd.tensor_tensor(w_lo[:, at], w_raw_b[:, :], f32(w_hi[:, at]), ALU.subtract).then_inc(wb_split, 1)
                pool.wait_ge(wb_split, n + 1)

            low_a(0, 0)
            load_a(0, 1)
            for k in range(KT):
                pool.wait_ge(ctx_hi_done, k + 1)
                nc.gpsimd.tensor_tensor(ctx_lo[:, k, :], ctx_raw[:, k, :], f32(ctx_hi[:, k, :]),
                                        ALU.subtract).then_inc(ctx_split, 1)
                if k == 0:
                    pool.wait_ge(half_set, 1)
                    pool.wait_ge(eps_done, 1)
                    nc.gpsimd.tensor_tensor(rstd[:, :], eps_var[:, :], minus_half[:, :], ALU.pow).then_inc(rstd_done, 1)
            low_a(1, 1)
            load_a(1, 0)
            low_b(0, 0)
            load_b(0, 1)
            low_b(1, 1)
            load_b(1, 0)

            def norm(g, b):
                pool.wait_ge(rinv_done, g * B + b + 1)
                r = rinv[b % 2][:, :].unsqueeze(2).to_broadcast([P, NE, P])
                nc.gpsimd.tensor_tensor(prob[b % 2][:, :, :], prob[b % 2][:, :, :], r, ALU.mult).then_inc(norm_done, 1)

            def lines(c, i):
                for key in POOL_LINES:
                    a, o = LINE[key]
                    nc.gpsimd.tensor_scalar(line[i][key][:, :], q_c[i][:, :], a, o, ALU.mult, ALU.add).then_inc(pool_lines, 1)

            def scale(c, i, ahead):
                pool.wait_ge(qc_done, c + (1 + ahead))
                pool.wait_ge(absmax_in, (c + 1) * 32)
                wait_past(pool, w_stored, c * 16)
                pool.wait_ge(env_done, c + 1)
                nc.gpsimd.tensor_tensor(w_out[:, :], line[i][8, 9][:, :], absmax[:, :], ALU.mult).then_inc(w_scaled, 1)

            def group(g, last):
                for b in range(B):
                    norm(g, b)
                    if not isinstance(g, int) or g * B + b >= 2:
                        scale(g * B + (b - 2), b % 2, 2)
                    else:
                        pool.wait_ge(qc_done, b + 1)
                    lines(g * B + b, b % 2)
                    if not last and b == 6:
                        low_a(g * 2 + 2, 0)
                        load_a(g + 1, 1)
                    if not last and b == 7:
                        low_a(g * 2 + 3, 1)
                if not last:
                    low_b(g * 2 + 2, 0)
                    load_b(g + 1, 1)
                    low_b(g * 2 + 3, 1)

            group(0, False)
            with pool.Fori(1, NG - 1) as g:
                load_a(g + 1, 0)
                load_b(g + 1, 0)
                group(g, False)
            group(NG - 1, True)
            for c in (CHUNKS - 2, CHUNKS - 1):
                scale(c, c % 2, 0)

            pool.wait_ge(eps_done, 2)
            nc.gpsimd.tensor_tensor(rstd[:, :], eps_var[:, :], minus_half[:, :], ALU.pow).then_inc(rstd_done, 1)

            with pool.Fori(0, MT // 2) as jj:
                for i in range(2):
                    pool.wait_ge(gu_hi_done, jj * 2 + (i + 1))
                    nc.gpsimd.tensor_tensor(gu_lo[i][:, :, :, :].rearrange("p a k m -> p (a k m)"), gu_raw[i][:, :],
                                            f32(gu_hi[i][:, :, :, :].rearrange("p a k m -> p (a k m)")), ALU.subtract).then_inc(gu_split, 1)
            with pool.Fori(0, MT // 2) as jj:
                for i in range(2):
                    pool.wait_ge(dn_hi_done, jj * 2 + (i + 1))
                    nc.gpsimd.tensor_tensor(dn_lo[i][:, :], dn_raw[i][:, :], f32(dn_hi[i][:, :]),
                                            ALU.subtract).then_inc(dn_split, 1)

        @block.scalar
        def _(act):
            def high_a(n, i):
                act.wait_ge(wa_in, (n + 1) * 16)
                at = slice(i * PIECE_A, (i + 1) * PIECE_A)
                nc.scalar.activation(w_hi[:, at], w_raw_a[:, :], ACT.Copy).then_inc(wa_hi, 1)

            def high_b(n, i):
                act.wait_ge(wb_in, (n + 1) * 16)
                at = slice(W_KV + W_Q + i * PIECE_B, W_KV + W_Q + (i + 1) * PIECE_B)
                nc.scalar.activation(w_hi[:, at], w_raw_b[:, :], ACT.Copy).then_inc(wb_hi, 1)

            act.wait_ge(line_at_set, len(ACT_LINES))
            act.wait_ge(gates_in, 16)
            nc.scalar.activation(gate[:, :], gate_raw[:, :], ACT.Tanh).then_inc(gate_done, 1)
            high_a(0, 0)
            act.wait_ge(ctx_in, 16)
            for k in range(KT):
                nc.scalar.activation(ctx_hi[:, k, :], ctx_raw[:, k, :], ACT.Copy).then_inc(ctx_hi_done, 1)
            ln_scalar(act, 0)
            high_a(1, 1)
            high_b(0, 0)
            high_b(1, 1)

            def split_hi(g, n):
                act.wait_ge(proj_done, nproj(g, n))
                nc.scalar.activation(proj_dst(n, k_hi, v_hi, q_hi), proj_ps[n % 2][:, :], ACT.Copy).then_inc(proj_hi, 1)

            def exps(g, b):
                act.wait_ge(bias_done, g * B + b + 1)
                for e in range(NE):
                    ins = nc.scalar.activation(prob[b % 2][:, e, :], prob[b % 2][:, e, :], ACT.Exp, bias=bias[b % 2][:, e:e + 1],
                                               scale=SCALE, accum_out=rsum[b % 2][:, e:e + 1])
                ins.then_inc(exp_done, 1)

            def pt_high(g, b):
                act.wait_ge(t_done, g * B + b + 1)
                nc.scalar.activation(flat(pt_hi[b % 2]), t_ps[:, :], ACT.Copy).then_inc(pt_hi_done, 1)

            def ot_high(g, b):
                act.wait_ge(o_done, g * B + b + 1)
                nc.scalar.activation(flat(ot_hi[b % 2]), o_ps[:, :], ACT.Copy).then_inc(ot_hi_done, 1)

            def lines(c, i):
                act.wait_ge(qc_done, c + 1)
                wait_past(act, w_scaled, c - 1)
                for key in ACT_LINES:
                    a, o = LINE[key]
                    fn = ACT.Relu if key == (8, 9) else ACT.Identity
                    nc.scalar.activation(line[i][key][:, :], q_c[i][:, :], fn, bias=line_at[:, key[0]:key[0] + 1],
                                         scale=a).then_inc(act_lines, 1)

            def group(g, last):
                for what, n in steps(last):
                    if what in "KVQ":
                        split_hi(g, n)
                    if what == "S":
                        exps(g, n)
                        if not isinstance(g, int) or g * B + n >= 1:
                            lines(g * B + (n - 1), (n - 1) % 2)
                    if what == "T":
                        pt_high(g, n)
                    if what == "O":
                        ot_high(g, n)
                    if not last and (what, n) == ("T", 6):
                        act.wait_ge(proj_done, nproj(g, 7))
                        high_a(g * 2 + 2, 0)
                    if not last and (what, n) == ("T", 7):
                        high_a(g * 2 + 3, 1)
                if not last:
                    act.wait_ge(y_done, g * B + B)
                    high_b(g * 2 + 2, 0)
                    high_b(g * 2 + 3, 1)

            for n in range(4):
                act.wait_ge(proj_done, n + 1)
                nc.scalar.activation(q_hi[:, n, :], proj_ps[n % 2][:, :], ACT.Copy).then_inc(proj_hi, 1)
            group(0, False)
            with act.Fori(1, NG - 1) as g:
                group(g, False)
            group(NG - 1, True)
            lines(CHUNKS - 1, (CHUNKS - 1) % 2)
            ln_scalar(act, LN_T)

            def high_gu(j, i, pair):
                act.wait_ge(gu_in[i], (pair + 1) * 16)
                wait_past(act, u_done, 2 * (j - 1))
                nc.scalar.activation(gu_hi[i][:, :, :, :].rearrange("p a k m -> p (a k m)"), gu_raw[i][:, :],
                                     ACT.Copy).then_inc(gu_hi_done, 1)

            def silus(j, i):
                for t in range(2):
                    act.wait_ge(g_done, 2 * j + (t + 1))
                    wait_past(act, h_done, 2 * j + (t - 1))
                    nc.scalar.activation(silu[t][:, :], banks[4 * i + t][:, :], ACT.Silu).then_inc(silu_done, 1)

            def hidden(jj, last):
                for i in range(2):
                    if not (last and i == 1):
                        high_gu(jj * 2 + (i + 1), 1 - i, jj + i)
                    silus(jj * 2 + i, i)

            high_gu(0, 0, 0)
            hidden(0, False)
            with act.Fori(1, MT // 2 - 1) as jj:
                hidden(jj, False)
            hidden(MT // 2 - 1, True)

            def down(jj):
                for i in range(2):
                    j = jj * 2 + i
                    act.wait_ge(dn_in[i], (jj + 1) * 16)
                    wait_past(act, down_done, j - 1)
                    nc.scalar.activation(dn_hi[i][:, :], dn_raw[i][:, :], ACT.Copy).then_inc(dn_hi_done, 1)
                    if isinstance(jj, int):
                        act.wait_ge(h_done, 2 * MT)
                    nc.scalar.activation(h_hi[i][:, :], h_cols(j), ACT.Copy).then_inc(hh_done, 1)

            down(0)
            with act.Fori(1, MT // 2) as jj:
                down(jj)

        @block.vector
        def _(dve):
            for key in ACT_LINES:
                nc.vector.memset(line_at[:, key[0]:key[0] + 1], LINE[key][1]).then_inc(line_at_set, 1)
            dve.wait_ge(x_in, 16)
            ln_vector(dve, 0, prob_tile)

            def proj_low(g, n):
                dve.wait_ge(proj_hi, nproj(g, n))
                nc.vector.tensor_tensor(proj_dst(n, k_lo, v_lo, q_lo), proj_ps[n % 2][:, :],
                                        f32(proj_dst(n, k_hi, v_hi, q_hi)), ALU.subtract).then_inc(proj_split, 1)

            def softmax(g, b):
                c = g * B + b
                dve.wait_ge(s_done, c + 1)
                nc.vector.tensor_tensor(prob[b % 2][:, :, :], s_ps[b % 2][:, :].rearrange("p (e k) -> p e k", e=NE),
                                        mask[:, :].unsqueeze(1).to_broadcast([P, NE, P]), ALU.add).then_inc(s_masked, 1)
                dve.wait_ge(s_masked, c + 1)
                nc.vector.tensor_reduce(bias[b % 2][:, :], prob[b % 2][:, :, :], AX_X, ALU.max).then_inc(max_done, 1)
                dve.wait_ge(max_done, c + 1)
                nc.vector.tensor_scalar(bias[b % 2][:, :], bias[b % 2][:, :], -SCALE, None, ALU.mult).then_inc(bias_done, 1)

            def rinvs(g, b):
                dve.wait_ge(exp_done, g * B + b + 1)
                nc.vector.reciprocal(rinv[b % 2][:, :], rsum[b % 2][:, :]).then_inc(rinv_done, 1)

            def codes(c, i):
                dve.wait_ge(q_in, (c + 1) * 16)
                nc.vector.tensor_scalar(q_c[i][:, :], q_raw[:, :], -7.0, None, ALU.add).then_inc(qc_done, 1)

            def envelope(c, i, part):
                up, low = line[i][8, 9], line[i][0, 1]

                if part == 0:
                    dve.wait_ge(act_lines, (c + 1) * 4)
                    nc.vector.tensor_tensor(up[:, :], up[:, :], line[i][14, 15][:, :], ALU.max).then_inc(env_step, 1)
                    dve.wait_ge(pool_lines, (c + 1) * 3)
                    nc.vector.tensor_tensor(low[:, :], low[:, :], line[i][2, 3][:, :], ALU.min).then_inc(env_step, 1)
                    dve.wait_ge(env_step, c * 6 + 1)
                    nc.vector.tensor_tensor(up[:, :], up[:, :], line[i][10, 11][:, :], ALU.max).then_inc(env_step, 1)
                    dve.wait_ge(env_step, c * 6 + 2)
                    nc.vector.tensor_tensor(low[:, :], low[:, :], line[i][4, 5][:, :], ALU.min).then_inc(env_step, 1)
                else:
                    dve.wait_ge(env_step, c * 6 + 3)
                    nc.vector.tensor_tensor(up[:, :], up[:, :], line[i][12, 13][:, :], ALU.max).then_inc(env_step, 1)
                    dve.wait_ge(env_step, c * 6 + 4)
                    nc.vector.scalar_tensor_tensor(low[:, :], q_c[i][:, :], LINE[6, 7][0], low[:, :],
                                                   ALU.mult, ALU.min).then_inc(env_step, 1)
                    dve.wait_ge(env_step, c * 6 + 6)
                    nc.vector.scalar_tensor_tensor(up[:, :], low[:, :], 0.0, up[:, :], ALU.min, ALU.add).then_inc(env_done, 1)

            def pt_low(g, b):
                dve.wait_ge(pt_hi_done, g * B + b + 1)
                nc.vector.tensor_tensor(flat(pt_lo[b % 2]), t_ps[:, :], f32(flat(pt_hi[b % 2])), ALU.subtract).then_inc(pt_split, 1)

            def ot_low(g, b):
                dve.wait_ge(ot_hi_done, g * B + b + 1)
                nc.vector.tensor_tensor(flat(ot_lo[b % 2]), o_ps[:, :], f32(flat(ot_hi[b % 2])), ALU.subtract).then_inc(ot_split, 1)

            def add_y(g, b):
                dve.wait_ge(y_done, g * B + b + 1)
                nc.vector.scalar_tensor_tensor(xs[:, b, :], y_ps[b % 2][:, :], gate[:, 0:1], xs[:, b, :],
                                               ALU.mult, ALU.add).then_inc(y_added, 1)

            def group(g, last):
                for what, n in steps(last):
                    if what in "KVQ":
                        proj_low(g, n)
                    if what == "S":
                        softmax(g, n)
                        some = not isinstance(g, int) or g * B + n >= 2
                        c = g * B + (n - 2)
                        if some:
                            envelope(c, n % 2, 0)
                        rinvs(g, n)
                        if some:
                            envelope(c, n % 2, 1)
                        codes(c + 2, n % 2)
                    if what == "T":
                        pt_low(g, n)
                    if what == "O":
                        ot_low(g, n)
                    if what == "Y":
                        add_y(g, n)

            for n in range(4):
                dve.wait_ge(proj_hi, n + 1)
                nc.vector.tensor_tensor(q_lo[:, n, :], proj_ps[n % 2][:, :], f32(q_hi[:, n, :]), ALU.subtract).then_inc(proj_split, 1)
            dve.wait_ge(gate_done, 1)
            dve.wait_ge(mask_done, 1)
            group(0, False)
            with dve.Fori(1, NG - 1) as g:
                group(g, False)
            group(NG - 1, True)
            for c in (CHUNKS - 2, CHUNKS - 1):
                envelope(c, c % 2, 0)
                envelope(c, c % 2, 1)
            dve.wait_ge(y_added, NG * B)
            dve.wait_ge(w_stored, 16 * CHUNKS)
            ln_vector(dve, LN_T, xn_tile)

            def hidden(jj):
                for i in range(2):
                    j = jj * 2 + i
                    for t in range(2):
                        dve.wait_ge(silu_done, 2 * j + (t + 1))
                        dve.wait_ge(u_done, 2 * j + (t + 1))
                        nc.vector.tensor_tensor(h_cols(j, t), banks[4 * i + 2 + t][:, :], silu[t][:, :],
                                                ALU.mult).then_inc(h_done, 1)

            with dve.Fori(0, MT // 2) as jj:
                hidden(jj)
            dve.wait_ge(h_done, 2 * MT)
            with dve.Fori(0, MT // 2) as jj:
                for i in range(2):
                    j = jj * 2 + i
                    dve.wait_ge(hh_done, j + 1)
                    nc.vector.tensor_tensor(h_lo[i][:, :], h_cols(j), f32(h_hi[i][:, :]), ALU.subtract).then_inc(h_split, 1)
            for b in range(B):
                dve.wait_ge(fin_ready, b + 1)
                nc.vector.scalar_tensor_tensor(xs[:, b, :], banks[b][:, :], gate[:, 1:2], xs[:, b, :],
                                               ALU.mult, ALU.add).then_inc(fin_done, 1)

        @block.tensor
        def _(pe):
            pe.wait_ge(ident_done, 1)
            ln_tensor(pe, 0, prob_tile)

            def product(dst, terms):
                n = len(terms)
                for i, (a_hi, a_lo, b_hi, b_lo) in enumerate(terms):
                    nc.tensor.matmul(dst, a_hi, b_lo, start=(i == 0), stop=False)
                    nc.tensor.matmul(dst, a_lo, b_hi, start=False, stop=False)
                    mm = nc.tensor.matmul(dst, a_hi, b_hi, start=False, stop=(i == n - 1))
                return mm

            def project(g, n, done_before):
                dst = proj_ps[n % 2]
                if n < 2:
                    cols = slice(n * HALF, (n + 1) * HALF)
                    mm = product(dst[:, :], [(wk(w_hi, k), wk(w_lo, k), ctx_hi[:, k, cols], ctx_lo[:, k, cols]) for k in range(KT)])
                elif n < 4:
                    for t in range(4):
                        toks = slice(((n - 2) * 4 + t) * P, ((n - 2) * 4 + t + 1) * P)
                        mm = product(dst[:, t * P:(t + 1) * P],
                                     [(ctx_hi[:, k, toks], ctx_lo[:, k, toks], wv(w_hi, k), wv(w_lo, k)) for k in range(KT)])
                else:
                    cols = slice(HALF, TOK) if n < 8 else slice(0, HALF)
                    mm = product(dst[:, :], [(wq(w_hi, k, n % 4), wq(w_lo, k, n % 4), ln_hi[:, k, cols], ln_lo[:, k, cols]) for k in range(KT)])
                mm.then_inc(proj_done, 1)

            def scores(g, b):
                wait_past(pe, s_masked, g * B + (b - 1))
                at = slice(b % 4 * P, (b % 4 + 1) * P)
                keys = slice(b * P, (b + 1) * P)
                for e in range(NE):
                    mm = product(s_ps[b % 2][:, e * P:(e + 1) * P],
                                 [(q_hi[:, e, at], q_lo[:, e, at], k_hi[:, keys], k_lo[:, keys])])
                mm.then_inc(s_done, 1)

            def turn(g, b):
                pe.wait_ge(norm_done, g * B + b + 1)
                wait_past(pe, pt_split, g * B + b)
                for e in range(NE):
                    mm = nc.tensor.transpose(t_ps[:, e * P:(e + 1) * P], prob[b % 2][:, e, :], ident[:, :])
                mm.then_inc(t_done, 1)

            def attend(g, b):
                pe.wait_ge(pt_split, g * B + b + 1)
                wait_past(pe, ot_split, g * B + b)
                product(o_ps[:, :], [(v_hi[:, b, :], v_lo[:, b, :], flat(pt_hi[b % 2]), flat(pt_lo[b % 2]))]).then_inc(o_done, 1)

            def out_project(g, b):
                pe.wait_ge(ot_split, g * B + b + 1)
                wait_past(pe, y_added, g * B + (b - 1))
                product(y_ps[b % 2][:, :], [(ot_hi[b % 2][:, e, :], ot_lo[b % 2][:, e, :], wd(w_hi, e), wd(w_lo, e))
                                            for e in range(NE)]).then_inc(y_done, 1)

            def group(g, last):
                for at, (what, n) in enumerate(steps(last)):
                    if what in "KVQ":
                        pe.wait_ge(proj_split, nproj(g, n) - 2)
                        if n == 8:
                            pe.wait_ge(wa_split, g * 2 + 4)
                        project(g, n, 0)
                    if what == "S":
                        if n == 0:
                            pe.wait_ge(proj_split, nproj(g, 1))
                        if n == 4:
                            pe.wait_ge(proj_split, nproj(g, 7))
                        scores(g, n)
                    if what == "T":
                        turn(g, n)
                    if what == "O":
                        if n in (0, 4):
                            pe.wait_ge(proj_split, nproj(g, 2 + n // 4))
                        attend(g, n)
                    if what == "Y":
                        if n == 0:
                            pe.wait_ge(wb_split, g * 2 + 2)
                        out_project(g, n)

            pe.wait_ge(ln_split, B)
            pe.wait_ge(wa_split, 2)
            for n in range(4):
                wait_past(pe, proj_split, n - 1)
                project(0, 8 + n, 0)
            pe.wait_ge(ctx_split, KT)
            group(0, False)
            with pe.Fori(1, NG - 1) as g:
                group(g, False)
            group(NG - 1, True)

            ln_tensor(pe, LN_T, xn_tile)
            pe.wait_ge(ln_split, 2 * B)

            def hidden(jj):
                for i in range(2):
                    j = jj * 2 + i
                    pe.wait_ge(gu_split, j + 1)
                    wait_past(pe, h_done, 2 * (j - 1))
                    for a, done in ((0, g_done), (1, u_done)):
                        for t in range(2):
                            cols = slice(t * HALF, (t + 1) * HALF)
                            product(banks[4 * i + 2 * a + t][:, :],
                                    [(gu_hi[i][:, a, k, :], gu_lo[i][:, a, k, :], ln_hi[:, k, cols], ln_lo[:, k, cols])
                                     for k in range(KT)]).then_inc(done, 1)

            hidden(0)
            with pe.Fori(1, MT // 2) as jj:
                hidden(jj)
            pe.wait_ge(h_done, 2 * MT)

            def down(jj, first, last):
                for i in range(2):
                    j = jj * 2 + i
                    pe.wait_ge(dn_split, j + 1)
                    pe.wait_ge(h_split, j + 1)
                    for b in range(B):
                        toks = slice(b * P, (b + 1) * P)
                        nc.tensor.matmul(banks[b][:, :], h_hi[i][:, toks], dn_lo[i][:, :], start=(first and i == 0), stop=False)
                        nc.tensor.matmul(banks[b][:, :], h_lo[i][:, toks], dn_hi[i][:, :], start=False, stop=False)
                        mm = nc.tensor.matmul(banks[b][:, :], h_hi[i][:, toks], dn_hi[i][:, :], start=False, stop=(last and i == 1))
                        if last and i == 1:
                            mm.then_inc(fin_ready, 1)
                    if not (last and i == 1):
                        mm.then_inc(down_done, 1)

            down(0, True, False)
            with pe.Fori(1, MT // 2 - 1) as jj:
                down(jj, False, False)
            down(MT // 2 - 1, False, True)


_INS = ['x', 'ctx_4096', 'g_xattn', 'g_ffn', 'L0_xattn_Wq', 'L0_xattn_Wk', 'L0_xattn_Wv', 'L0_xattn_Wd',
        'L0_ffn_gate_q', 'L0_ffn_gate_absmax', 'L0_ffn_up_q', 'L0_ffn_up_absmax', 'L0_ffn_down_q', 'L0_ffn_down_absmax']


def lay_out(x, ctx_4096, g_xattn, g_ffn, L0_xattn_Wq, L0_xattn_Wk, L0_xattn_Wv, L0_xattn_Wd,
            L0_ffn_gate_q, L0_ffn_gate_absmax, L0_ffn_up_q, L0_ffn_up_absmax, L0_ffn_down_q, L0_ffn_down_absmax):
    import numpy as np
    kv = [w.reshape(NG, P, KT, P).transpose(0, 3, 2, 1).reshape(NG, P, KT * P) for w in (L0_xattn_Wk, L0_xattn_Wv)]
    wq = L0_xattn_Wq.reshape(NG, NE * P, KT, P).transpose(0, 3, 2, 1).reshape(NG, P, KT * NE * P)
    wd = L0_xattn_Wd.reshape(D, NG, NE, P).transpose(1, 3, 2, 0).reshape(NG, P, NE * D)
    gu = [q.reshape(MT, P, KT, P).transpose(3, 0, 2, 1).reshape(P, MT, D) for q in (L0_ffn_gate_q, L0_ffn_up_q)]
    down = L0_ffn_down_q.reshape(D, MT, P).transpose(2, 1, 0)
    gu_absmax = [a.reshape(MT, P, KT, 2).transpose(3, 0, 2, 1).reshape(2, MT, D) for a in (L0_ffn_gate_absmax, L0_ffn_up_absmax)]
    down_absmax = L0_ffn_down_absmax.reshape(D, MT, 2).transpose(2, 1, 0)
    return {
        "x": x,
        "ctx_t": ctx_4096.reshape(TOK, D).T,
        "gates": np.concatenate([g_xattn, g_ffn]),
        "w_groups": np.concatenate([*kv, wq, wd], axis=2),
        "ff_q": np.concatenate([*gu, down], axis=2).reshape(P, FF),
        "ff_absmax": np.concatenate([*gu_absmax, down_absmax], axis=2).reshape(2, FF),
    }


def kernel(**inputs):
    import numpy as _np
    import concourse.bacc as _bacc
    from concourse.bass_utils import run_bass_kernel_spmd as _run

    nc = _bacc.Bacc("TRN2", target_bir_lowering=False, num_devices=1, dynamic_dma_scratch_size=8192)
    laid = {k: _np.ascontiguousarray(v) for k, v in lay_out(**{n: _np.asarray(inputs[n]) for n in _INS}).items()}
    args = {k: nc.dram_tensor(f"in_{k}", v.shape, mybir.dt.from_np(v.dtype), kind="ExternalInput").ap() for k, v in laid.items()}
    out = nc.dram_tensor("out_0_dram", (B, S, D), F32, kind="ExternalOutput").ap()
    flamingo(nc, **args, out=out)
    r = _run(nc, [{f"in_{k}": v for k, v in laid.items()}], core_ids=[0])
    return r.results[0]["out_0_dram"]
```

```python
from contextlib import ExitStack

import concourse.bass as bass
from concourse import mybir

ALU = mybir.AluOpType
ACT = mybir.ActivationFunctionType
F32 = mybir.dt.float32
F32R = mybir.dt.float32r
I32 = mybir.dt.int32
AX_X = mybir.AxisListType.X

P = 128
B, S, D = 8, 128, 512
TOK = B * S
HALF = TOK // 2
KT = D // P
NG, NE = 8, 4
M = 1792
MT = M // P
SCALE = float(P) ** -0.5
EPS = 1e-5
MASKED = -3.0e38

W_Q = KT * NE * P
W_KV = 2 * KT * P
W_D = NE * D
W_G = W_KV + W_Q + W_D
PIECE = (W_Q + W_KV) // 2
PIECES = 4
PIECE_COLS = ((W_Q + W_KV, W_D // 2), (W_Q + W_KV + W_D // 2, W_D // 2), (0, PIECE), (PIECE, PIECE))

FF_J = 3 * D
FF = MT * FF_J
CHUNKS = NG * B
CH = FF // CHUNKS

LN_T = B
T_LAG, O_LAG, Y_LAG, ADD_LAG, TURN_LAG = 1, 2, 3, 4, 6
PROJ_AT = {1: (0,), 2: (1,), 3: (2, 3, 4, 5), 7: (6, 7, 8, 9, 10, 11)}
PROJ, PROJ_OWN, PROJ_AHEAD = 12, 6, 6
CHUNKS_AT = {1: (0,), 2: (1,), 3: (2, 3), 4: (4,), 7: (5, 6, 7)}

LINE = {
    (8, 9): (0.08134990185499191, -0.001769605907611549),
    (10, 11): (0.0918029248714447, -0.029296472668647766),
    (12, 13): (0.12190712988376617, -0.16882582008838654),
    (14, 15): (0.2770431637763977, -1.2163453102111816),
    (0, 1): (0.30380716919898987, 1.1266502141952515),
    (2, 3): (0.1301555335521698, 0.12570463120937347),
    (4, 5): (0.09966793656349182, 0.014562436379492283),
    (6, 7): (0.09105003625154495, 0.0),
}
ACT_LINES = ((8, 9), (14, 15), (0, 1), (10, 11))
POOL_LINES = ((2, 3), (4, 5), (12, 13))


def proj_tiles(b, last):
    return tuple(n for n in PROJ_AT.get(b, ()) if n < PROJ_OWN or not last)


def wait_past(engine, semaphore, count):
    if not isinstance(count, int) or count > 0:
        engine.wait_ge(semaphore, count)


def flamingo(nc, x, ctx_t, gates, w_groups, ff_q, ff_absmax, out):
    ff_w = nc.dram_tensor("ff_dequantised", (P, FF), F32, kind="Internal").ap()
    with ExitStack() as stack:
        def sb(name, shape, dt=F32, on=None):
            return (on or stack).enter_context(nc.sbuf_tensor(name, shape, dt))

        def sem(name):
            return stack.enter_context(nc.semaphore(name))

        banks = [stack.enter_context(nc.psum_tensor(f"bank{i}", [P, D], F32)) for i in range(8)]
        proj_ps, s_ps, t_ps, o_ps, y_ps = banks[0:2], banks[2:4], banks[4], banks[5], banks[6:8]

        g_ps, u_ps = (banks[2:4], banks[6:8]), (banks[4:6], banks[0:2])

        xs = sb("xs", [P, B, D])
        ln_hi = sb("ln_hi", [P, KT, TOK], F32R)
        ln_lo = sb("ln_lo", [P, KT, TOK], F32R)
        xn = [sb(f"xn{i}", [P, D]) for i in range(2)]
        ident = sb("ident", [P, P])
        mask = sb("mask", [P, P])
        gate_raw = sb("gate_raw", [P, 2])
        gate = sb("gate", [P, 2])
        stats = sb("stats", [P, B, 6])
        mv = sb("mv", [P, B, 2])
        rstd = sb("rstd", [P, B])
        eps_var = sb("eps_var", [P, B])
        minus_half = sb("minus_half", [P, B])
        line_at = sb("line_at", [P, 16])

        attn = ExitStack()
        ctx_hi = sb("ctx_hi", [P, KT, TOK], F32R, attn)
        ctx_lo = sb("ctx_lo", [P, KT, TOK], F32R, attn)
        w_raw = [sb(f"w_raw{i}", [P, PIECE], F32, attn) for i in range(2)]
        w_hi = sb("w_hi", [P, W_G], F32R, attn)
        w_lo = sb("w_lo", [P, W_G], F32R, attn)
        k_hi = sb("k_hi", [P, TOK], F32R, attn)
        k_lo = sb("k_lo", [P, TOK], F32R, attn)
        v_hi = sb("v_hi", [P, B, P], F32R, attn)
        v_lo = sb("v_lo", [P, B, P], F32R, attn)
        q_hi = sb("q_hi", [P, NE, HALF], F32R, attn)
        q_lo = sb("q_lo", [P, NE, HALF], F32R, attn)
        prob = [sb(f"prob{i}", [P, NE, P], F32, attn) for i in range(2)]
        bias = [sb(f"bias{i}", [P, NE], F32, attn) for i in range(2)]
        rsum = [sb(f"rsum{i}", [P, NE], F32, attn) for i in range(2)]
        rinv = [sb(f"rinv{i}", [P, NE], F32, attn) for i in range(2)]
        q_raw = sb("q_raw", [P, CH], I32, attn)
        absmax = sb("absmax", [P, CH], F32, attn)
        q_c = [sb(f"q_c{i}", [P, CH], F32, attn) for i in range(2)]
        line = [{k: sb(f"line{k[0]}_{i}", [P, CH], F32, attn) for k in LINE if k != (6, 7)} for i in range(2)]
        w_out = sb("w_out", [P, CH], F32, attn)
        with ExitStack() as first:
            ctx_raw = sb("ctx_raw", [P, KT, TOK], F32, first)
        pt_hi = [sb(f"pt_hi{i}", [P, NE, P], F32R, attn) for i in range(2)]
        pt_lo = [sb(f"pt_lo{i}", [P, NE, P], F32R, attn) for i in range(2)]
        ot_hi = [sb(f"ot_hi{i}", [P, NE, P], F32R, attn) for i in range(2)]
        ot_lo = [sb(f"ot_lo{i}", [P, NE, P], F32R, attn) for i in range(2)]
        attn.close()

        ffs = ExitStack()
        gu_raw = [sb(f"gu_raw{i}", [P, 2 * D], F32, ffs) for i in range(2)]
        gu_hi = [sb(f"gu_hi{i}", [P, 2, KT, P], F32R, ffs) for i in range(2)]
        gu_lo = [sb(f"gu_lo{i}", [P, 2, KT, P], F32R, ffs) for i in range(2)]
        silu = [sb(f"silu{i}", [P, HALF], F32, ffs) for i in range(2)]
        dn_raw = [sb(f"dn_raw{i}", [P, D], F32, ffs) for i in range(2)]
        h = sb("h", [P, MT, TOK], F32, ffs)
        dn_hi = [sb(f"dn_hi{i}", [P, D], F32R, ffs) for i in range(2)]
        dn_lo = [sb(f"dn_lo{i}", [P, D], F32R, ffs) for i in range(2)]
        h_hi = [sb(f"h_hi{i}", [P, TOK], F32R, ffs) for i in range(2)]
        h_lo = [sb(f"h_lo{i}", [P, TOK], F32R, ffs) for i in range(2)]
        ffs.close()

        x_in, ctx_in, gates_in = [sem(f"x_in{b}") for b in range(B)], sem("ctx_in"), sem("gates_in")
        w_in = [sem(f"w_in{i}") for i in range(2)]
        q_in, absmax_in, w_stored = sem("q_in"), sem("absmax_in"), sem("w_stored")
        gu_in = [sem(f"gu_in{i}") for i in range(2)]
        dn_in = [sem(f"dn_in{i}") for i in range(2)]
        out_done = sem("out_done")
        ident_zero, ident_done, mask_zero, mask_done = sem("ident_zero"), sem("ident_done"), sem("mask_zero"), sem("mask_done")
        half_set, line_at_set, gate_done = sem("half_set"), sem("line_at_set"), sem("gate_done")
        stats_done, mv_done, eps_done, rstd_done = sem("stats_done"), sem("mv_done"), sem("eps_done"), sem("rstd_done")
        xn_done, ln_turned, ln_hi_done, ln_split = sem("xn_done"), sem("ln_turned"), sem("ln_hi_done"), sem("ln_split")
        ctx_hi_done, ctx_split = sem("ctx_hi_done"), sem("ctx_split")
        w_hi_done, w_split = sem("w_hi_done"), sem("w_split")
        proj_done, proj_hi, proj_split = sem("proj_done"), sem("proj_hi"), sem("proj_split")
        s_done, s_masked, max_done, bias_done = sem("s_done"), sem("s_masked"), sem("max_done"), sem("bias_done")
        exp_done, rinv_done, norm_done = sem("exp_done"), sem("rinv_done"), sem("norm_done")
        t_done, pt_hi_done, pt_split = sem("t_done"), sem("pt_hi_done"), sem("pt_split")
        o_done, ot_hi_done, ot_split = sem("o_done"), sem("ot_hi_done"), sem("ot_split")
        y_done, y_added = sem("y_done"), sem("y_added")
        qc_done, act_lines, pool_lines = sem("qc_done"), sem("act_lines"), sem("pool_lines")
        env_step, env_done, w_scaled = sem("env_step"), sem("env_done"), sem("w_scaled")
        gu_hi_done, gu_split = sem("gu_hi_done"), sem("gu_split")
        g_done, u_done, silu_done, h_done = sem("g_done"), sem("u_done"), sem("silu_done"), sem("h_done")
        dn_hi_done, dn_split, hh_done, h_split = sem("dn_hi_done"), sem("dn_split"), sem("hh_done"), sem("h_split")
        down_done, fin_ready, fin_done = sem("down_done"), sem("fin_ready"), sem("fin_done")

        def f32(ap):
            return ap.bitcast(F32)

        def flat(tile):
            return tile[:, :, :].rearrange("p a b -> p (a b)")

        def flat4(tile):
            return tile[:, :, :, :].rearrange("p a k m -> p (a k m)")

        def h_cols(j, t=None):
            at, n = (j * TOK, TOK) if t is None else (j * TOK + t * HALF, HALF)
            return h[:, :, :].rearrange("p j t -> p (j t)")[:, bass.ds(at, n)]

        def wk(w, kt):
            return w[:, W_Q + kt * P:W_Q + (kt + 1) * P]

        def wv(w, kt):
            return w[:, W_Q + (KT + kt) * P:W_Q + (KT + kt + 1) * P]

        def wq(w, kt, e):
            at = kt * NE * P + e * P
            return w[:, at:at + P]

        def wd(w, e):
            at = W_KV + W_Q + e * D
            return w[:, at:at + D]

        def proj_dst(n, v, k, q):
            if n < 2:
                return v[:, n * 4:(n + 1) * 4, :].rearrange("p b d -> p (b d)")
            if n < 10:
                return q[:, (n - 2) % 4, :]
            return k[:, (n - 10) * HALF:(n - 9) * HALF]

        def nproj(g, n):
            return g * PROJ + (PROJ_AHEAD + n + 1)

        def npiece(g, p):
            return g * PIECES + (p + 3)

        def piece(p, raw, w):
            at, n = PIECE_COLS[p]
            return raw[p % 2][:, 0:n], w[:, at:at + n]

        def batch_of(g, b, lag):
            n = g * B + (b - lag)
            return None if isinstance(n, int) and not 0 <= n < NG * B else n

        def ln_stats(dve, done, b):
            if done:
                dve.wait_ge(y_added, (NG - 1) * B + b + 1)
            else:
                dve.wait_ge(x_in[b], 16)
            nc.vector.bn_stats(stats[:, b, :], xs[:, b, :]).then_inc(stats_done, 1)
            dve.wait_ge(stats_done, done + b + 1)
            nc.vector.bn_aggr(mv[:, b, :], stats[:, b, :]).then_inc(mv_done, 1)
            dve.wait_ge(mv_done, done + b + 1)
            nc.vector.tensor_scalar(eps_var[:, b:b + 1], mv[:, b, 1:2], EPS, None, ALU.add).then_inc(eps_done, 1)

        def ln_power(pool, done, b):
            pool.wait_ge(eps_done, done + b + 1)
            nc.gpsimd.tensor_tensor(rstd[:, b:b + 1], eps_var[:, b:b + 1], minus_half[:, b:b + 1], ALU.pow).then_inc(rstd_done, 1)

        def ln_norm(dve, done, b):
            dve.wait_ge(rstd_done, done + b + 1)
            wait_past(dve, ln_turned, done + b - 1)
            nc.vector.tensor_scalar(xn[b % 2][:, :], xs[:, b, :], mv[:, b, 0:1], rstd[:, b:b + 1],
                                    ALU.subtract, ALU.mult).then_inc(xn_done, 1)

        def ln_turn(pe, done, b):
            pe.wait_ge(xn_done, done + b + 1)
            wait_past(pe, ln_split, done + b - 1)
            for k in range(KT):
                mm = nc.tensor.transpose(banks[b % 2][:, k * P:(k + 1) * P], xn[b % 2][:, k * P:(k + 1) * P], ident[:, :])
            mm.then_inc(ln_turned, 1)

        def ln_high(act, done, b):
            act.wait_ge(ln_turned, done + b + 1)
            nc.scalar.activation(ln_hi[:, :, b * P:(b + 1) * P], banks[b % 2][:, :].rearrange("p (k t) -> p k t", k=KT),
                                 ACT.Copy).then_inc(ln_hi_done, 1)

        def ln_low(dve, done, b):
            dve.wait_ge(ln_hi_done, done + b + 1)
            at = slice(b * P, (b + 1) * P)
            nc.vector.tensor_tensor(ln_lo[:, :, at], banks[b % 2][:, :].rearrange("p (k t) -> p k t", k=KT),
                                    f32(ln_hi[:, :, at]), ALU.subtract).then_inc(ln_split, 1)

        block = stack.enter_context(nc.Block())

        @block.sync
        def _(sp):
            for b in range(B):
                sp.dma_start(xs[:, b, :], x[b]).then_inc(x_in[b], 16)
            sp.dma_start(gate_raw[:, :], gates.partition_broadcast(P)).then_inc(gates_in, 16)
            sp.dma_start(ctx_raw[:, :, :], ctx_t.rearrange("(k p) t -> p k t", p=P)).then_inc(ctx_in, 16)

            def load_q(c):
                wait_past(sp, qc_done, c)
                sp.dma_start(q_raw[:, :], ff_q[:, bass.ds(c * CH, CH)]).then_inc(q_in, 16)

            def load_absmax(c):
                for i in range(2):
                    sp.dma_start(absmax[64 * i:64 * (i + 1), :],
                                 ff_absmax[i, bass.ds(c * CH, CH)].partition_broadcast(64)).then_inc(absmax_in, 16)

            def store(c):
                sp.wait_ge(w_scaled, c + 1)
                sp.dma_start(ff_w[:, bass.ds(c * CH, CH)], w_out[:, :]).then_inc(w_stored, 16)

            load_q(0)
            load_absmax(0)
            load_q(1)
            load_q(2)
            with sp.Fori(0, CHUNKS - 3) as c:
                load_q(c + 3)
                store(c)
                load_absmax(c + 1)
            for c in range(CHUNKS - 3, CHUNKS):
                store(c)
                if c + 1 < CHUNKS:
                    load_absmax(c + 1)
            sp.wait_ge(w_stored, 16 * CHUNKS)
            sp.wait_ge(proj_done, nproj(NG - 1, PROJ_OWN - 1))

            def load_gu(j, i, free):
                if free:
                    sp.wait_ge(gu_split, j - 1)
                sp.dma_start(gu_raw[i][:, :], ff_w[:, bass.ds(j * FF_J, 2 * D)]).then_inc(gu_in[i], 16)

            def load_dn(j, i, free):
                if free:
                    sp.wait_ge(dn_split, j - 1)
                sp.dma_start(dn_raw[i][:, :], ff_w[:, bass.ds(j * FF_J + 2 * D, D)]).then_inc(dn_in[i], 16)

            for i in range(2):
                load_gu(i, i, False)
                load_dn(i, i, False)
            with sp.Fori(1, MT // 2) as jj:
                for i in range(2):
                    load_gu(jj * 2 + i, i, True)
            with sp.Fori(1, MT // 2) as jj:
                for i in range(2):
                    load_dn(jj * 2 + i, i, True)
            for b in range(B):
                sp.wait_ge(fin_done, b + 1)
                sp.dma_start(out[b], xs[:, b, :]).then_inc(out_done, 16)
            sp.wait_ge(out_done, 16 * B)

        @block.gpsimd
        def _(pool):
            def load_w(g, p):
                at, n = PIECE_COLS[p]
                pool.dma_start(w_raw[p % 2][:, 0:n], w_groups[g + 1 if p >= 2 else g, :, at:at + n]).then_inc(w_in[p % 2], 16)

            def low_w(g, p):
                raw, lo = piece(p, w_raw, w_lo)
                pool.wait_ge(w_hi_done, npiece(g, p))
                nc.gpsimd.tensor_tensor(lo, raw, f32(piece(p, w_raw, w_hi)[1]), ALU.subtract).then_inc(w_split, 1)

            def next_w(g, p, last):
                low_w(g, p)
                if not last:
                    pool.wait_ge(w_split, npiece(g, p))
                    load_w(g + 1 if p >= 2 else g, (p + 2) % PIECES)

            def norm(n, i):
                pool.wait_ge(rinv_done, n + 1)
                nc.gpsimd.tensor_tensor(prob[i][:, :, :], prob[i][:, :, :], rinv[i][:, :].unsqueeze(2).to_broadcast([P, NE, P]),
                                        ALU.mult).then_inc(norm_done, 1)

            def scale(c, i, ahead):
                pool.wait_ge(qc_done, c + (1 + ahead))
                pool.wait_ge(absmax_in, (c + 1) * 32)
                wait_past(pool, w_stored, c * 16)
                pool.wait_ge(env_done, c + 1)
                nc.gpsimd.tensor_tensor(w_out[:, :], line[i][8, 9][:, :], absmax[:, :], ALU.mult).then_inc(w_scaled, 1)

            def chunk(c, i):
                if isinstance(c, int) and c == 0:
                    pool.wait_ge(qc_done, 1)
                else:
                    scale(c - 1, 1 - i, 1)
                for key in POOL_LINES:
                    a, o = LINE[key]
                    nc.gpsimd.tensor_scalar(line[i][key][:, :], q_c[i][:, :], a, o, ALU.mult, ALU.add).then_inc(pool_lines, 1)

            def slot(g, b, last):
                if b < B:
                    norm(g * B + b, b % 2)
                for k in CHUNKS_AT.get(b, ()):
                    if b == 3:
                        next_w(g, k - 2, last)
                    chunk(g * B + k, k % 2)
                if b in (4, 5) and not last:
                    next_w(g, b - 2, last)
                if last and 0 <= b - ADD_LAG < B:
                    ln_power(pool, LN_T, b - ADD_LAG)

            def low_gu(j, i):
                pool.wait_ge(gu_hi_done, j + 1)
                nc.gpsimd.tensor_tensor(flat4(gu_lo[i]), gu_raw[i][:, :], f32(flat4(gu_hi[i])), ALU.subtract).then_inc(gu_split, 1)

            def low_dn(j, i):
                pool.wait_ge(dn_hi_done, j + 1)
                nc.gpsimd.tensor_tensor(dn_lo[i][:, :], dn_raw[i][:, :], f32(dn_hi[i][:, :]), ALU.subtract).then_inc(dn_split, 1)

            load_w(-1, 2)
            load_w(-1, 3)
            nc.gpsimd.memset(ident[:, :], 0.0).then_inc(ident_zero, 1)
            nc.gpsimd.memset(mask[:, :], 0.0).then_inc(mask_zero, 1)
            nc.gpsimd.memset(minus_half[:, :], -0.5).then_inc(half_set, 1)
            pool.wait_ge(ident_zero, 1)
            nc.gpsimd.affine_select(out=ident[:, :], in_=ident[:, :], compare_op=ALU.not_equal, fill=1.0, base=0,
                                    pattern=[[-1, P]], channel_multiplier=1).then_inc(ident_done, 1)
            pool.wait_ge(mask_zero, 1)
            nc.gpsimd.affine_select(out=mask[:, :], in_=mask[:, :], compare_op=ALU.is_ge, fill=MASKED, base=0,
                                    pattern=[[-1, P]], channel_multiplier=1).then_inc(mask_done, 1)
            pool.wait_ge(half_set, 1)
            for b in range(B):
                ln_power(pool, 0, b)
            for p in range(2):
                pool.wait_ge(w_split, p + 1)
                load_w(0, p)
            for k in range(2):
                pool.wait_ge(ctx_hi_done, k + 1)
                nc.gpsimd.tensor_tensor(ctx_lo[:, k, :], ctx_raw[:, k, :], f32(ctx_hi[:, k, :]), ALU.subtract).then_inc(ctx_split, 1)

            for b in range(B):
                slot(0, b, False)
            with pool.Fori(1, NG - 1) as g:
                for b in range(B):
                    slot(g, b, False)
            for b in range(B + ADD_LAG):
                if b == B:
                    scale(CHUNKS - 1, (CHUNKS - 1) % 2, 0)
                if b >= B + 2:
                    low_gu(b - B - 2, b - B - 2)
                slot(NG - 1, b, True)

            with pool.Fori(1, MT // 2) as jj:
                for i in range(2):
                    low_gu(jj * 2 + i, i)
            with pool.Fori(0, MT // 2) as jj:
                for i in range(2):
                    low_dn(jj * 2 + i, i)

        @block.scalar
        def _(act):
            def high_w(g, p):
                raw, hi = piece(p, w_raw, w_hi)
                act.wait_ge(w_in[p % 2], g * (PIECES // 2 * 16) + (p // 2 + 2) * 16)
                if p < 2:
                    wait_past(act, y_done, g * B)
                else:
                    wait_past(act, proj_done, nproj(g, PROJ_OWN - 1) if not isinstance(g, int) or g >= 0 else 0)
                nc.scalar.activation(hi, raw, ACT.Copy).then_inc(w_hi_done, 1)

            def proj_high(g, n):
                act.wait_ge(proj_done, nproj(g, n))
                nc.scalar.activation(proj_dst(n, v_hi, k_hi, q_hi), proj_ps[n % 2][:, :], ACT.Copy).then_inc(proj_hi, 1)

            def exps(n, i):
                act.wait_ge(bias_done, n + 1)
                for e in range(NE):
                    ins = nc.scalar.activation(prob[i][:, e, :], prob[i][:, e, :], ACT.Exp, bias=bias[i][:, e:e + 1],
                                               scale=SCALE, accum_out=rsum[i][:, e:e + 1])
                ins.then_inc(exp_done, 1)

            def pt_high(n, i):
                act.wait_ge(t_done, n + 1)
                nc.scalar.activation(flat(pt_hi[i]), t_ps[:, :], ACT.Copy).then_inc(pt_hi_done, 1)

            def ot_high(n, i):
                act.wait_ge(o_done, n + 1)
                nc.scalar.activation(flat(ot_hi[i]), o_ps[:, :], ACT.Copy).then_inc(ot_hi_done, 1)

            def chunk(c, i):
                act.wait_ge(qc_done, c + 1)
                wait_past(act, w_scaled, c - 1)
                for key in ACT_LINES:
                    fn = ACT.Relu if key == (8, 9) else ACT.Identity
                    nc.scalar.activation(line[i][key][:, :], q_c[i][:, :], fn, bias=line_at[:, key[0]:key[0] + 1],
                                         scale=LINE[key][0]).then_inc(act_lines, 1)

            def slot(g, b, last):
                if (n := batch_of(g, b, O_LAG)) is not None:
                    ot_high(n, b % 2)
                if (n := batch_of(g, b, T_LAG)) is not None:
                    pt_high(n, (b - 1) % 2)
                if b < B:
                    exps(g * B + b, b % 2)
                tiles = proj_tiles(b, last)
                chunks = CHUNKS_AT.get(b, ())
                for k in range(max(len(tiles), len(chunks))):
                    if b == 3 and k < 2:
                        high_w(g, k)
                    if k < len(tiles):
                        proj_high(g, tiles[k])
                    if k < len(chunks):
                        chunk(g * B + chunks[k], chunks[k] % 2)
                if b in (4, 5) and not last:
                    high_w(g, b - 2)
                if last and 0 <= b - TURN_LAG < B:
                    ln_high(act, LN_T, b - TURN_LAG)

            act.wait_ge(line_at_set, len(ACT_LINES))
            for b in range(B):
                ln_high(act, 0, b)
                if b in (2, 5):
                    high_w(-1, 2 + b // 3)
            act.wait_ge(ctx_in, 16)
            for k in range(KT):
                nc.scalar.activation(ctx_hi[:, k, :], ctx_raw[:, k, :], ACT.Copy).then_inc(ctx_hi_done, 1)
            act.wait_ge(gates_in, 16)
            nc.scalar.activation(gate[:, :], gate_raw[:, :], ACT.Tanh).then_inc(gate_done, 1)
            for n in range(PROJ_AHEAD):
                proj_high(-1, PROJ_OWN + n)

            for b in range(B):
                slot(0, b, False)
            with act.Fori(1, NG - 1) as g:
                for b in range(B):
                    slot(g, b, False)

            def high_gu(j, i, pair):
                act.wait_ge(gu_in[i], (pair + 1) * 16)
                wait_past(act, u_done, 2 * (j - 1))
                nc.scalar.activation(flat4(gu_hi[i]), gu_raw[i][:, :], ACT.Copy).then_inc(gu_hi_done, 1)

            for b in range(B + TURN_LAG):
                if B + 1 <= b < B + 3:
                    high_gu(b - B - 1, b - B - 1, 0)
                slot(NG - 1, b, True)

            def silus(j, i):
                for t in range(2):
                    act.wait_ge(g_done, 2 * j + (t + 1))
                    wait_past(act, h_done, 2 * j + (t - 1))
                    nc.scalar.activation(silu[t][:, :], g_ps[i][t][:, :], ACT.Silu).then_inc(silu_done, 1)

            def down_parts(jj, i):
                j = jj * 2 + i
                act.wait_ge(dn_in[i], (jj + 1) * 16)
                wait_past(act, down_done, j - 1)
                nc.scalar.activation(dn_hi[i][:, :], dn_raw[i][:, :], ACT.Copy).then_inc(dn_hi_done, 1)
                if isinstance(jj, int):
                    act.wait_ge(h_done, 2 * j + 2)
                nc.scalar.activation(h_hi[i][:, :], h_cols(j), ACT.Copy).then_inc(hh_done, 1)

            silus(0, 0)
            silus(1, 1)
            with act.Fori(1, MT // 2) as jj:
                for i in range(2):
                    high_gu(jj * 2 + i, i, jj)
                for i in range(2):
                    silus(jj * 2 + i, i)
            act.wait_ge(h_done, 2 * MT)
            for i in range(2):
                down_parts(0, i)
            with act.Fori(1, MT // 2) as jj:
                for i in range(2):
                    down_parts(jj, i)

        @block.vector
        def _(dve):
            def proj_low(g, n):
                dve.wait_ge(proj_hi, nproj(g, n))
                nc.vector.tensor_tensor(proj_dst(n, v_lo, k_lo, q_lo), proj_ps[n % 2][:, :],
                                        f32(proj_dst(n, v_hi, k_hi, q_hi)), ALU.subtract).then_inc(proj_split, 1)

            def softmax(n, i):
                dve.wait_ge(s_done, n + 1)
                nc.vector.tensor_tensor(prob[i][:, :, :], s_ps[i][:, :].rearrange("p (e k) -> p e k", e=NE),
                                        mask[:, :].unsqueeze(1).to_broadcast([P, NE, P]), ALU.add).then_inc(s_masked, 1)
                dve.wait_ge(s_masked, n + 1)
                nc.vector.tensor_reduce(bias[i][:, :], prob[i][:, :, :], AX_X, ALU.max).then_inc(max_done, 1)
                dve.wait_ge(max_done, n + 1)
                nc.vector.tensor_scalar(bias[i][:, :], bias[i][:, :], -SCALE, None, ALU.mult).then_inc(bias_done, 1)

            def rinvs(n, i):
                dve.wait_ge(exp_done, n + 1)
                nc.vector.reciprocal(rinv[i][:, :], rsum[i][:, :]).then_inc(rinv_done, 1)

            def pt_low(n, i):
                dve.wait_ge(pt_hi_done, n + 1)
                nc.vector.tensor_tensor(flat(pt_lo[i]), t_ps[:, :], f32(flat(pt_hi[i])), ALU.subtract).then_inc(pt_split, 1)

            def ot_low(n, i):
                dve.wait_ge(ot_hi_done, n + 1)
                nc.vector.tensor_tensor(flat(ot_lo[i]), o_ps[:, :], f32(flat(ot_hi[i])), ALU.subtract).then_inc(ot_split, 1)

            def add_y(n, b):
                dve.wait_ge(y_done, n + 1)
                nc.vector.scalar_tensor_tensor(xs[:, b, :], y_ps[b % 2][:, :], gate[:, 0:1], xs[:, b, :],
                                               ALU.mult, ALU.add).then_inc(y_added, 1)

            def codes(c, i):
                dve.wait_ge(q_in, (c + 1) * 16)
                nc.vector.tensor_scalar(q_c[i][:, :], q_raw[:, :], -7.0, None, ALU.add).then_inc(qc_done, 1)

            def envelope(c, i):
                up, low = line[i][8, 9], line[i][0, 1]
                dve.wait_ge(act_lines, (c + 1) * 4)
                nc.vector.tensor_tensor(up[:, :], up[:, :], line[i][14, 15][:, :], ALU.max).then_inc(env_step, 1)
                dve.wait_ge(pool_lines, (c + 1) * 3)
                nc.vector.tensor_tensor(low[:, :], low[:, :], line[i][2, 3][:, :], ALU.min).then_inc(env_step, 1)
                dve.wait_ge(env_step, c * 6 + 1)
                nc.vector.tensor_tensor(up[:, :], up[:, :], line[i][10, 11][:, :], ALU.max).then_inc(env_step, 1)
                dve.wait_ge(env_step, c * 6 + 2)
                nc.vector.tensor_tensor(low[:, :], low[:, :], line[i][4, 5][:, :], ALU.min).then_inc(env_step, 1)
                dve.wait_ge(env_step, c * 6 + 3)
                nc.vector.tensor_tensor(up[:, :], up[:, :], line[i][12, 13][:, :], ALU.max).then_inc(env_step, 1)
                dve.wait_ge(env_step, c * 6 + 4)
                nc.vector.scalar_tensor_tensor(low[:, :], q_c[i][:, :], LINE[6, 7][0], low[:, :],
                                               ALU.mult, ALU.min).then_inc(env_step, 1)
                dve.wait_ge(env_step, c * 6 + 6)
                nc.vector.scalar_tensor_tensor(up[:, :], low[:, :], 0.0, up[:, :], ALU.min, ALU.add).then_inc(env_done, 1)

            def chunk(c, i):
                envelope(c, i)
                if not isinstance(c, int) or c + 2 < CHUNKS:
                    codes(c + 2, i)

            def slot(g, b, last):
                if b < B:
                    softmax(g * B + b, b % 2)
                if (n := batch_of(g, b, O_LAG)) is not None:
                    ot_low(n, b % 2)
                if (n := batch_of(g, b, T_LAG)) is not None:
                    pt_low(n, (b - 1) % 2)
                if (n := batch_of(g, b, ADD_LAG)) is not None:
                    add_y(n, (b - ADD_LAG) % B)
                if b < B:
                    rinvs(g * B + b, b % 2)
                if last and 0 <= b - ADD_LAG < B:
                    ln_stats(dve, LN_T, b - ADD_LAG)
                if last and 0 <= b - ADD_LAG - 1 < B:
                    ln_norm(dve, LN_T, b - ADD_LAG - 1)
                if last and 0 <= b - TURN_LAG - 1 < B:
                    ln_low(dve, LN_T, b - TURN_LAG - 1)
                tiles = proj_tiles(b, last)
                chunks = CHUNKS_AT.get(b, ())
                for k in range(max(len(tiles), len(chunks))):
                    if k < len(tiles):
                        proj_low(g, tiles[k])
                    if k < len(chunks):
                        chunk(g * B + chunks[k], chunks[k] % 2)

            def low_first_w(p):
                raw, lo = piece(p, w_raw, w_lo)
                dve.wait_ge(w_hi_done, p - 1)
                nc.vector.tensor_tensor(lo, raw, f32(piece(p, w_raw, w_hi)[1]), ALU.subtract).then_inc(w_split, 1)

            for key in ACT_LINES:
                nc.vector.memset(line_at[:, key[0]:key[0] + 1], LINE[key][1]).then_inc(line_at_set, 1)
            for b in range(B + 3):
                if b < B:
                    ln_stats(dve, 0, b)
                if 1 <= b <= B:
                    ln_norm(dve, 0, b - 1)
                if b >= 3:
                    ln_low(dve, 0, b - 3)
                if b in (6, 9):
                    low_first_w(2 + b // 9)
            for c in range(2):
                codes(c, c)
            for k in range(2, KT):
                dve.wait_ge(ctx_hi_done, k + 1)
                nc.vector.tensor_tensor(ctx_lo[:, k, :], ctx_raw[:, k, :], f32(ctx_hi[:, k, :]), ALU.subtract).then_inc(ctx_split, 1)
            for n in range(PROJ_AHEAD):
                proj_low(-1, PROJ_OWN + n)
            dve.wait_ge(gate_done, 1)
            dve.wait_ge(mask_done, 1)
            for b in range(B):
                slot(0, b, False)
            with dve.Fori(1, NG - 1) as g:
                for b in range(B):
                    slot(g, b, False)
            for b in range(B + TURN_LAG + 1):
                slot(NG - 1, b, True)
            dve.wait_ge(w_stored, 16 * CHUNKS)

            with dve.Fori(0, MT // 2) as jj:
                for i in range(2):
                    j = jj * 2 + i
                    for t in range(2):
                        dve.wait_ge(silu_done, 2 * j + (t + 1))
                        dve.wait_ge(u_done, 2 * j + (t + 1))
                        nc.vector.tensor_tensor(h_cols(j, t), u_ps[i][t][:, :], silu[t][:, :], ALU.mult).then_inc(h_done, 1)
            dve.wait_ge(h_done, 2 * MT)
            with dve.Fori(0, MT // 2) as jj:
                for i in range(2):
                    j = jj * 2 + i
                    dve.wait_ge(hh_done, j + 1)
                    nc.vector.tensor_tensor(h_lo[i][:, :], h_cols(j), f32(h_hi[i][:, :]), ALU.subtract).then_inc(h_split, 1)
            for b in range(B):
                dve.wait_ge(fin_ready, b + 1)
                nc.vector.scalar_tensor_tensor(xs[:, b, :], banks[b][:, :], gate[:, 1:2], xs[:, b, :],
                                               ALU.mult, ALU.add).then_inc(fin_done, 1)

        @block.tensor
        def _(pe):
            def product(dst, terms):
                for i, (a_hi, a_lo, b_hi, b_lo) in enumerate(terms):
                    nc.tensor.matmul(dst, a_hi, b_lo, start=(i == 0), stop=False)
                    nc.tensor.matmul(dst, a_lo, b_hi, start=False, stop=False)
                    mm = nc.tensor.matmul(dst, a_hi, b_hi, start=False, stop=(i == len(terms) - 1))
                return mm

            def project(g, n):
                pe.wait_ge(proj_split, nproj(g, n) - 2) if not (isinstance(g, int) and nproj(g, n) <= 2) else None
                dst = proj_ps[n % 2]
                if n < 2:
                    for t in range(4):
                        toks = slice((n * 4 + t) * P, (n * 4 + t + 1) * P)
                        mm = product(dst[:, t * P:(t + 1) * P],
                                     [(ctx_hi[:, k, toks], ctx_lo[:, k, toks], wv(w_hi, k), wv(w_lo, k)) for k in range(KT)])
                elif n < 10:
                    cols = slice(HALF, TOK) if n < PROJ_OWN else slice(0, HALF)
                    e = (n - 2) % 4
                    mm = product(dst[:, :], [(wq(w_hi, k, e), wq(w_lo, k, e), ln_hi[:, k, cols], ln_lo[:, k, cols]) for k in range(KT)])
                else:
                    cols = slice((n - 10) * HALF, (n - 9) * HALF)
                    mm = product(dst[:, :], [(wk(w_hi, k), wk(w_lo, k), ctx_hi[:, k, cols], ctx_lo[:, k, cols]) for k in range(KT)])
                mm.then_inc(proj_done, 1)

            def scores(n, b):
                wait_past(pe, s_masked, n - 1)
                at = slice(b % 4 * P, (b % 4 + 1) * P)
                keys = slice(b * P, (b + 1) * P)
                for e in range(NE):
                    mm = product(s_ps[b % 2][:, e * P:(e + 1) * P],
                                 [(q_hi[:, e, at], q_lo[:, e, at], k_hi[:, keys], k_lo[:, keys])])
                mm.then_inc(s_done, 1)

            def turn(n, i):
                pe.wait_ge(norm_done, n + 1)
                wait_past(pe, pt_split, n)
                for e in range(NE):
                    mm = nc.tensor.transpose(t_ps[:, e * P:(e + 1) * P], prob[i][:, e, :], ident[:, :])
                mm.then_inc(t_done, 1)

            def attend(n, b):
                pe.wait_ge(pt_split, n + 1)
                wait_past(pe, ot_split, n)
                product(o_ps[:, :], [(v_hi[:, b, :], v_lo[:, b, :], flat(pt_hi[b % 2]), flat(pt_lo[b % 2]))]).then_inc(o_done, 1)

            def out_project(n, b):
                pe.wait_ge(ot_split, n + 1)
                wait_past(pe, y_added, n - 1)
                product(y_ps[b % 2][:, :], [(ot_hi[b % 2][:, e, :], ot_lo[b % 2][:, e, :], wd(w_hi, e), wd(w_lo, e))
                                            for e in range(NE)]).then_inc(y_done, 1)

            def slot(g, b, last):
                if b < B:
                    if b == 0:
                        pe.wait_ge(proj_split, nproj(g, -1))
                    if b == 4:
                        pe.wait_ge(proj_split, nproj(g, PROJ_OWN - 1))
                    scores(g * B + b, b)
                if (n := batch_of(g, b, O_LAG)) is not None:
                    if b - O_LAG in (0, 4):
                        pe.wait_ge(proj_split, nproj(g, (b - O_LAG) // 4))
                    attend(n, (b - O_LAG) % B)
                if (n := batch_of(g, b, T_LAG)) is not None:
                    turn(n, (b - T_LAG) % 2)
                for t in proj_tiles(b, last):
                    if t == PROJ_OWN:
                        pe.wait_ge(w_split, npiece(g, 3))
                    project(g, t)
                if last and 0 <= b - TURN_LAG < 5:
                    ln_turn(pe, LN_T, b - TURN_LAG)
                if (n := batch_of(g, b, Y_LAG)) is not None:
                    if b == Y_LAG:
                        pe.wait_ge(w_split, npiece(g, 1))
                    out_project(n, (b - Y_LAG) % B)

            pe.wait_ge(ident_done, 1)
            for b in range(B):
                ln_turn(pe, 0, b)
            pe.wait_ge(ln_split, B)
            pe.wait_ge(w_split, 2)
            for n in range(PROJ_AHEAD):
                if n == NE:
                    pe.wait_ge(ctx_split, KT)
                project(-1, PROJ_OWN + n)
            for b in range(B):
                slot(0, b, False)
            with pe.Fori(1, NG - 1) as g:
                for b in range(B):
                    slot(g, b, False)
            for b in range(B + Y_LAG):
                slot(NG - 1, b, True)

            def hidden_tile(i, a, t):
                cols = slice(t * HALF, (t + 1) * HALF)
                product((g_ps, u_ps)[a][i][t][:, :], [(gu_hi[i][:, a, k, :], gu_lo[i][:, a, k, :], ln_hi[:, k, cols], ln_lo[:, k, cols])
                                                      for k in range(KT)]).then_inc((g_done, u_done)[a], 1)

            def hidden(j, i):
                pe.wait_ge(gu_split, j + 1)
                wait_past(pe, h_done, 2 * (j - 1))
                for a in range(2):
                    for t in range(2):
                        hidden_tile(i, a, t)

            pe.wait_ge(gu_split, 1)
            pe.wait_ge(ln_split, LN_T + B // 2)
            hidden_tile(0, 0, 0)
            ln_turn(pe, LN_T, 5)
            hidden_tile(0, 1, 0)
            ln_turn(pe, LN_T, 6)
            ln_turn(pe, LN_T, 7)
            pe.wait_ge(ln_split, LN_T + B)
            hidden_tile(0, 0, 1)
            hidden_tile(0, 1, 1)
            hidden(1, 1)
            with pe.Fori(1, MT // 2) as jj:
                for i in range(2):
                    hidden(jj * 2 + i, i)
            pe.wait_ge(h_done, 2 * MT)

            def down(jj, first, last):
                for i in range(2):
                    j = jj * 2 + i
                    pe.wait_ge(dn_split, j + 1)
                    pe.wait_ge(h_split, j + 1)
                    for b in range(B):
                        toks = slice(b * P, (b + 1) * P)
                        nc.tensor.matmul(banks[b][:, :], h_hi[i][:, toks], dn_lo[i][:, :], start=(first and i == 0), stop=False)
                        nc.tensor.matmul(banks[b][:, :], h_lo[i][:, toks], dn_hi[i][:, :], start=False, stop=False)
                        mm = nc.tensor.matmul(banks[b][:, :], h_hi[i][:, toks], dn_hi[i][:, :], start=False, stop=(last and i == 1))
                        if last and i == 1:
                            mm.then_inc(fin_ready, 1)
                    if not (last and i == 1):
                        mm.then_inc(down_done, 1)

            down(0, True, False)
            with pe.Fori(1, MT // 2 - 1) as jj:
                down(jj, False, False)
            down(MT // 2 - 1, False, True)


_INS = ['x', 'ctx_4096', 'g_xattn', 'g_ffn', 'L0_xattn_Wq', 'L0_xattn_Wk', 'L0_xattn_Wv', 'L0_xattn_Wd',
        'L0_ffn_gate_q', 'L0_ffn_gate_absmax', 'L0_ffn_up_q', 'L0_ffn_up_absmax', 'L0_ffn_down_q', 'L0_ffn_down_absmax']


def lay_out(x, ctx_4096, g_xattn, g_ffn, L0_xattn_Wq, L0_xattn_Wk, L0_xattn_Wv, L0_xattn_Wd,
            L0_ffn_gate_q, L0_ffn_gate_absmax, L0_ffn_up_q, L0_ffn_up_absmax, L0_ffn_down_q, L0_ffn_down_absmax):
    import numpy as np
    kv = [w.reshape(NG, P, KT, P).transpose(0, 3, 2, 1).reshape(NG, P, KT * P) for w in (L0_xattn_Wk, L0_xattn_Wv)]
    wq = L0_xattn_Wq.reshape(NG, NE * P, KT, P).transpose(0, 3, 2, 1).reshape(NG, P, KT * NE * P)
    wd = L0_xattn_Wd.reshape(D, NG, NE, P).transpose(1, 3, 2, 0).reshape(NG, P, NE * D)
    gu = [q.reshape(MT, P, KT, P).transpose(3, 0, 2, 1).reshape(P, MT, D) for q in (L0_ffn_gate_q, L0_ffn_up_q)]
    down = L0_ffn_down_q.reshape(D, MT, P).transpose(2, 1, 0)
    gu_absmax = [a.reshape(MT, P, KT, 2).transpose(3, 0, 2, 1).reshape(2, MT, D) for a in (L0_ffn_gate_absmax, L0_ffn_up_absmax)]
    down_absmax = L0_ffn_down_absmax.reshape(D, MT, 2).transpose(2, 1, 0)
    return {
        "x": x,
        "ctx_t": ctx_4096.reshape(TOK, D).T,
        "gates": np.concatenate([g_xattn, g_ffn]),
        "w_groups": np.concatenate([wq, *kv, wd], axis=2),
        "ff_q": np.concatenate([*gu, down], axis=2).reshape(P, FF),
        "ff_absmax": np.concatenate([*gu_absmax, down_absmax], axis=2).reshape(2, FF),
    }


def kernel(**inputs):
    import numpy as _np
    import concourse.bacc as _bacc
    from concourse.bass_utils import run_bass_kernel_spmd as _run

    nc = _bacc.Bacc("TRN2", target_bir_lowering=False, num_devices=1, dynamic_dma_scratch_size=8192)
    laid = {k: _np.ascontiguousarray(v) for k, v in lay_out(**{n: _np.asarray(inputs[n]) for n in _INS}).items()}
    args = {k: nc.dram_tensor(f"in_{k}", v.shape, mybir.dt.from_np(v.dtype), kind="ExternalInput").ap() for k, v in laid.items()}
    out = nc.dram_tensor("out_0_dram", (B, S, D), F32, kind="ExternalOutput").ap()
    flamingo(nc, **args, out=out)
    r = _run(nc, [{f"in_{k}": v for k, v in laid.items()}], core_ids=[0])
    return r.results[0]["out_0_dram"]
```

```python
from contextlib import ExitStack

import concourse.bass as bass
from concourse import mybir

ALU = mybir.AluOpType
ACT = mybir.ActivationFunctionType
F32 = mybir.dt.float32
F32R = mybir.dt.float32r
I32 = mybir.dt.int32
AX_X = mybir.AxisListType.X

P = 128
B, S, D = 8, 128, 512
TOK = B * S
HALF = TOK // 2
KT = D // P
NG, NE = 8, 4
M = 1792
MT = M // P
SCALE = float(P) ** -0.5
EPS = 1e-5
MASKED = -3.0e38

W_QH = KT * 2 * P
W_K = KT * P
W_D = NE * D
W_G = 2 * W_QH + W_K + W_D
W_V = KT * 2 * P
PIECE_COLS = {"q0": (0, W_QH), "q1": (W_QH, W_QH), "k": (2 * W_QH, W_K), "d0": (W_G - W_D, W_D // 2), "d1": (W_G - W_D // 2, W_D // 2),
              "v0": (W_G, W_V // 2), "v1": (W_G + W_V // 2, W_V // 2)}
PIECE = W_QH

FF_J = 3 * D
FF = MT * FF_J
CHUNKS = (NG - 1) * B
CH = FF // CHUNKS

TURN, TURNS = 2 * B, NG // 2
T_LAG, O_LAG, Y_LAG, TURN_LAG = 1, 2, 3, 5
LN_T = B
TILES = ((0, "q0", 1), (0, "k", 1), (1, "q1", 1), (1, "v", 1), (2, "q0", 2), (3, "q1", 2), (3, "v", 2), (4, "q0", 3),
         (5, "q1", 3), (5, "k", 0), (6, "q0", 0), (6, "v", 3), (7, "q1", 0),
         (8, "q0", 1), (9, "q1", 1), (9, "k", 1), (10, "q0", 2), (11, "q1", 2), (12, "q0", 3),
         (13, "q1", 3), (13, "k", 0), (14, "q0", 0), (14, "v", 0), (15, "q1", 0))
PROJ, PROJ_AHEAD = len(TILES), 4
FIRST_TILES = (21, 23, 20, 22)
PIECES = ((2, "d0"), (2, "d1"), (3, "k"), (4, "q0"), (5, "q1"),
          (10, "d0"), (10, "d1"), (11, "k"), (11, "v0"), (12, "v1"), (12, "q0"), (13, "q1"))
PIECES_AHEAD = 5
FIRST_PIECES = (10, 11, 7, 8, 9)
PAIR = 2 * P

FIRST_HALVES = ((0, 0), (1, 0), (0, 1), (1, 1))
DOWN_ORDER = (2, 3, 4, 5, 6, 7, 0, 1)

LINE = {
    (8, 9): (0.08134990185499191, -0.001769605907611549),
    (10, 11): (0.0918029248714447, -0.029296472668647766),
    (12, 13): (0.12190712988376617, -0.16882582008838654),
    (14, 15): (0.2770431637763977, -1.2163453102111816),
    (0, 1): (0.30380716919898987, 1.1266502141952515),
    (2, 3): (0.1301555335521698, 0.12570463120937347),
    (4, 5): (0.09966793656349182, 0.014562436379492283),
    (6, 7): (0.09105003625154495, 0.0),
}
ACT_LINES = ((8, 9), (14, 15), (0, 1), (10, 11))
POOL_LINES = ((2, 3), (4, 5), (12, 13))


def latest(things, slot, name, *more):
    found = [n for n, (at, *what) in enumerate(things) if what == [name, *more]]
    return max([n for n in found if things[n][0] < slot], default=found[-1] - len(things))


def slot_things(things, s, ahead, last):
    return tuple(n for n, thing in enumerate(things) if thing[0] == s and (n < len(things) - ahead or not last))


def slot_tiles(s, last):
    return slot_things(TILES, s, PROJ_AHEAD, last)


def slot_pieces(s, last):
    return slot_things(PIECES, s, PIECES_AHEAD, last)


def has_chunk(s, last):
    return s < (B if last else TURN)


def second_tile(turn, s, last):
    if s == 0:
        return () if isinstance(turn, int) and turn == 0 else tuple(n - PROJ for n in slot_tiles(TURN - 1, False)[1:])
    return slot_tiles(s - 1, last)[1:]


def seq_buffer(seq, t):
    return seq % 2 if isinstance(seq, int) else t


def wait_past(engine, semaphore, count):
    if not isinstance(count, int) or count > 0:
        engine.wait_ge(semaphore, count)


def flamingo(nc, x, ctx_t, gates, w_groups, w_v, ff_q, ff_absmax, out):
    ff_w = nc.dram_tensor("ff_dequantised", (P, FF), F32, kind="Internal").ap()
    with ExitStack() as stack:
        def sb(name, shape, dt=F32, on=None):
            return (on or stack).enter_context(nc.sbuf_tensor(name, shape, dt))

        def sem(name):
            return stack.enter_context(nc.semaphore(name))

        banks = [stack.enter_context(nc.psum_tensor(f"bank{i}", [P, D], F32)) for i in range(8)]
        proj_ps, s_ps, t_ps, o_ps, y_ps = banks[0:2], banks[2:4], banks[4], banks[5], banks[6:8]

        g_ps, u_ps = (banks[2:4], banks[6:8]), (banks[4:6], banks[0:2])

        xs = sb("xs", [P, B, D])
        ln_hi = sb("ln_hi", [P, KT, TOK], F32R)
        ln_lo = sb("ln_lo", [P, KT, TOK], F32R)
        xn = [sb(f"xn{i}", [P, D]) for i in range(2)]
        ident = sb("ident", [P, P])
        mask = sb("mask", [P, P])
        gate_raw = sb("gate_raw", [P, 2])
        gate = sb("gate", [P, 2])
        stats = sb("stats", [P, B, 6])
        mv = sb("mv", [P, B, 2])
        rstd = sb("rstd", [P, B])
        eps_var = sb("eps_var", [P, B])
        minus_half = sb("minus_half", [P, B])
        line_at = sb("line_at", [P, 16])

        attn = ExitStack()
        ctx_hi = sb("ctx_hi", [P, KT, TOK], F32R, attn)
        ctx_lo = sb("ctx_lo", [P, KT, TOK], F32R, attn)
        w_raw = [sb(f"w_raw{i}", [P, PIECE], F32, attn) for i in range(2)]
        w_hi = sb("w_hi", [P, W_G + W_V], F32R, attn)
        w_lo = sb("w_lo", [P, W_G + W_V], F32R, attn)
        k_hi = sb("k_hi", [P, TOK], F32R, attn)
        k_lo = sb("k_lo", [P, TOK], F32R, attn)
        v_hi = sb("v_hi", [P, B, 2, P], F32R, attn)
        v_lo = sb("v_lo", [P, B, 2, P], F32R, attn)
        q_hi = sb("q_hi", [P, 2, NE, PAIR], F32R, attn)
        q_lo = sb("q_lo", [P, 2, NE, PAIR], F32R, attn)
        prob = [sb(f"prob{i}", [P, NE, P], F32, attn) for i in range(2)]
        bias = [sb(f"bias{i}", [P, NE], F32, attn) for i in range(2)]
        rsum = [sb(f"rsum{i}", [P, NE], F32, attn) for i in range(2)]
        rinv = [sb(f"rinv{i}", [P, NE], F32, attn) for i in range(2)]
        q_raw = sb("q_raw", [P, CH], I32, attn)
        absmax = sb("absmax", [P, CH], F32, attn)
        q_c = [sb(f"q_c{i}", [P, CH], F32, attn) for i in range(2)]
        w_out = sb("w_out", [P, CH], F32, attn)
        with ExitStack() as first:
            ctx_raw = sb("ctx_raw", [P, KT, TOK], F32, first)
        line = [{k: sb(f"line{k[0]}_{i}", [P, CH], F32, attn) for k in LINE if k != (6, 7)} for i in range(2)]
        pt_hi = sb("pt_hi", [P, NE, P], F32R, attn)
        pt_lo = sb("pt_lo", [P, NE, P], F32R, attn)
        ot_hi = sb("ot_hi", [P, NE, P], F32R, attn)
        ot_lo = sb("ot_lo", [P, NE, P], F32R, attn)
        attn.close()

        ffs = ExitStack()
        gu_raw = [sb(f"gu_raw{i}", [P, 2 * D], F32, ffs) for i in range(2)]
        gu_hi = [sb(f"gu_hi{i}", [P, 2, KT, P], F32R, ffs) for i in range(2)]
        gu_lo = [sb(f"gu_lo{i}", [P, 2, KT, P], F32R, ffs) for i in range(2)]
        silu = [sb(f"silu{i}", [P, HALF], F32, ffs) for i in range(2)]
        dn_raw = [sb(f"dn_raw{i}", [P, D], F32, ffs) for i in range(2)]
        h = sb("h", [P, MT, TOK], F32, ffs)
        dn_hi = [sb(f"dn_hi{i}", [P, D], F32R, ffs) for i in range(2)]
        dn_lo = [sb(f"dn_lo{i}", [P, D], F32R, ffs) for i in range(2)]
        h_hi = [sb(f"h_hi{i}", [P, TOK], F32R, ffs) for i in range(2)]
        h_lo = [sb(f"h_lo{i}", [P, TOK], F32R, ffs) for i in range(2)]
        ffs.close()

        x_in, ctx_in, gates_in = [sem(f"x_in{b}") for b in range(B)], [sem(f"ctx_in{k}") for k in range(KT)], sem("gates_in")
        w_in = [sem(f"w_in{i}") for i in range(2)]
        q_in, absmax_in, w_stored = sem("q_in"), sem("absmax_in"), sem("w_stored")
        gu_in = [sem(f"gu_in{i}") for i in range(2)]
        dn_in = [sem(f"dn_in{i}") for i in range(2)]
        out_done = sem("out_done")
        ident_zero, ident_done, mask_zero, mask_done = sem("ident_zero"), sem("ident_done"), sem("mask_zero"), sem("mask_done")
        half_set, line_at_set, gate_done = sem("half_set"), sem("line_at_set"), sem("gate_done")
        stats_done, mv_done, eps_done, rstd_done = sem("stats_done"), sem("mv_done"), sem("eps_done"), sem("rstd_done")
        xn_done, ln_turned, ln_hi_done, ln_split = sem("xn_done"), sem("ln_turned"), sem("ln_hi_done"), sem("ln_split")
        ctx_hi_done, ctx_split = sem("ctx_hi_done"), sem("ctx_split")
        w_hi_done, w_split = sem("w_hi_done"), sem("w_split")
        proj_done, proj_hi, proj_split = sem("proj_done"), sem("proj_hi"), sem("proj_split")
        s_done, s_masked, max_done, bias_done = sem("s_done"), sem("s_masked"), sem("max_done"), sem("bias_done")
        exp_done, rinv_done, norm_done = sem("exp_done"), sem("rinv_done"), sem("norm_done")
        t_done, pt_hi_done, pt_split = sem("t_done"), sem("pt_hi_done"), sem("pt_split")
        o_done, ot_hi_done, ot_split = sem("o_done"), sem("ot_hi_done"), sem("ot_split")
        y_done, y_added = sem("y_done"), sem("y_added")
        qc_done, act_lines, pool_lines = sem("qc_done"), sem("act_lines"), sem("pool_lines")
        env_step, env_done, w_scaled = sem("env_step"), sem("env_done"), sem("w_scaled")
        gu_hi_done, gu_split = sem("gu_hi_done"), sem("gu_split")
        g_done, u_done, silu_done, h_done = sem("g_done"), sem("u_done"), sem("silu_done"), sem("h_done")
        dn_hi_done, dn_split, hh_done, h_split = sem("dn_hi_done"), sem("dn_split"), sem("hh_done"), sem("h_split")
        down_done, fin_ready, fin_done = sem("down_done"), sem("fin_ready"), sem("fin_done")

        def f32(ap):
            return ap.bitcast(F32)

        def flat(tile):
            return tile[:, :, :].rearrange("p a b -> p (a b)")

        def flat4(tile):
            return tile[:, :, :, :].rearrange("p a k m -> p (a k m)")

        def h_cols(j, t=None):
            at, n = (j * TOK, TOK) if t is None else (j * TOK + t * HALF, HALF)
            return h[:, :, :].rearrange("p j t -> p (j t)")[:, bass.ds(at, n)]

        def wq(w, kt, e):
            at = e // 2 * W_QH + (kt * 2 + e % 2) * P
            return w[:, at:at + P]

        def wk(w, kt):
            return w[:, 2 * W_QH + kt * P:2 * W_QH + (kt + 1) * P]

        def wv(w, kt):
            return w[:, W_G + kt * PAIR:W_G + (kt + 1) * PAIR]

        def wd(w, e):
            at = W_G - W_D + e * D
            return w[:, at:at + D]

        def proj_dst(n, v, k, q):
            _, name, at = TILES[n]
            if name == "v":
                return v[:, at * 2:(at + 1) * 2, :, :].rearrange("p b g d -> p (b g d)")
            if name == "k":
                return k[:, at * HALF:(at + 1) * HALF]
            heads = int(name[1]) * 2
            return q[:, at % 2, heads:heads + 2, :].rearrange("p e t -> p (e t)")

        def made(turn, n):
            return turn * PROJ + (PROJ_AHEAD + n)

        def proj_bank(n):
            return proj_ps[(PROJ_AHEAD + n) % 2]

        def nproj(turn, n):
            return turn * PROJ + (PROJ_AHEAD + n + 1)

        def npiece(turn, p):
            return turn * len(PIECES) + (PIECES_AHEAD + p + 1)

        def piece(p, w):
            at, n = PIECE_COLS[PIECES[p][1]]
            return w[:, at:at + n]

        def piece_raw(p, i):
            return w_raw[i][:, 0:PIECE_COLS[PIECES[p][1]][1]]

        def before(turn, s, lag):
            n = turn * TURN + (s - lag)
            return (None if isinstance(n, int) and not 0 <= n < NG * B else n), (s - lag) % B

        def ln_bank(done, b):
            return (proj_ps if done else y_ps)[b % 2]

        def ln_stats(dve, done, b):
            if done:
                dve.wait_ge(y_added, (NG - 1) * B + b + 1)
            else:
                dve.wait_ge(x_in[b], 16)
            nc.vector.bn_stats(stats[:, b, :], xs[:, b, :]).then_inc(stats_done, 1)
            dve.wait_ge(stats_done, done + b + 1)
            nc.vector.bn_aggr(mv[:, b, :], stats[:, b, :]).then_inc(mv_done, 1)
            dve.wait_ge(mv_done, done + b + 1)
            nc.vector.tensor_scalar(eps_var[:, b:b + 1], mv[:, b, 1:2], EPS, None, ALU.add).then_inc(eps_done, 1)

        def ln_power(pool, done, b):
            pool.wait_ge(eps_done, done + b + 1)
            nc.gpsimd.tensor_tensor(rstd[:, b:b + 1], eps_var[:, b:b + 1], minus_half[:, b:b + 1], ALU.pow).then_inc(rstd_done, 1)

        def ln_norm(dve, done, b):
            dve.wait_ge(rstd_done, done + b + 1)
            wait_past(dve, ln_turned, done + b - 1)
            nc.vector.tensor_scalar(xn[b % 2][:, :], xs[:, b, :], mv[:, b, 0:1], rstd[:, b:b + 1],
                                    ALU.subtract, ALU.mult).then_inc(xn_done, 1)

        def ln_turn(pe, done, b):
            pe.wait_ge(xn_done, done + b + 1)
            wait_past(pe, ln_split, done + b - 1)
            for k in range(KT):
                mm = nc.tensor.transpose(ln_bank(done, b)[:, k * P:(k + 1) * P], xn[b % 2][:, k * P:(k + 1) * P], ident[:, :])
            mm.then_inc(ln_turned, 1)

        def ln_high(act, done, b):
            act.wait_ge(ln_turned, done + b + 1)
            nc.scalar.activation(ln_hi[:, :, b * P:(b + 1) * P], ln_bank(done, b)[:, :].rearrange("p (k t) -> p k t", k=KT),
                                 ACT.Copy).then_inc(ln_hi_done, 1)

        def ln_low(dve, done, b):
            dve.wait_ge(ln_hi_done, done + b + 1)
            at = slice(b * P, (b + 1) * P)
            nc.vector.tensor_tensor(ln_lo[:, :, at], ln_bank(done, b)[:, :].rearrange("p (k t) -> p k t", k=KT),
                                    f32(ln_hi[:, :, at]), ALU.subtract).then_inc(ln_split, 1)

        block = stack.enter_context(nc.Block())

        @block.sync
        def _(sp):
            def load_x(b):
                sp.dma_start(xs[:, b, :], x[b]).then_inc(x_in[b], 16)

            def load_w(turn, p, i):
                slot, name = PIECES[p]
                if name[0] == "v":
                    src, at = w_v, turn * W_V + (W_V + int(name[1]) * (W_V // 2))
                else:
                    group = slot // B + (name[0] != "d")
                    src, at = w_groups, turn * (2 * W_G) + (group * W_G + PIECE_COLS[name][0])
                sp.dma_start(piece_raw(p, i), src[:, bass.ds(at, PIECE_COLS[name][1])]).then_inc(w_in[i], 16)

            def next_w(turn, s, last):
                for p in slot_pieces(s - 1, last):
                    if last and p + 2 >= len(PIECES) - PIECES_AHEAD:
                        continue
                    sp.wait_ge(w_split, npiece(turn, p))
                    load_w(turn + (p + 2) // len(PIECES), (p + 2) % len(PIECES), (PIECES_AHEAD + p) % 2)

            def load_ctx(k):
                sp.dma_start(ctx_raw[:, k, :], ctx_t[k * P:(k + 1) * P, :]).then_inc(ctx_in[k], 16)

            def load_q(c):
                wait_past(sp, qc_done, c)
                sp.dma_start(q_raw[:, :], ff_q[:, bass.ds(c * CH, CH)]).then_inc(q_in, 16)

            def load_absmax(c):
                for i in range(2):
                    sp.dma_start(absmax[64 * i:64 * (i + 1), :],
                                 ff_absmax[i, bass.ds(c * CH, CH)].partition_broadcast(64)).then_inc(absmax_in, 16)

            def store(c):
                sp.wait_ge(w_scaled, c + 1)
                sp.dma_start(ff_w[:, bass.ds(c * CH, CH)], w_out[:, :]).then_inc(w_stored, 16)

            def slot(turn, s, last):
                if not last or has_chunk(s + 1, last):
                    load_q(turn * TURN + (s + 1))
                next_w(turn, s, last)
                n, _ = before(turn, s, 2)
                if n is not None and has_chunk(s - 2, last):
                    store(n)
                    if not last or has_chunk(s - 1, last):
                        load_absmax(turn * TURN + (s - 1))

            sp.dma_start(gate_raw[:, :], gates.partition_broadcast(P)).then_inc(gates_in, 16)
            for b in range(2):
                load_x(b)
            for i in range(2):
                load_w(-1, FIRST_PIECES[i], i)
            for b in range(2, 4):
                load_x(b)
            for k in range(KT):
                load_ctx(k)
            for i in range(2):
                sp.wait_ge(w_split, i + 1)
                load_w(-1, FIRST_PIECES[2 + i], i)
            for b in range(4, B):
                load_x(b)
            sp.wait_ge(w_split, 3)
            load_w(-1, FIRST_PIECES[4], 0)
            load_q(0)
            load_absmax(0)
            for p in range(2):
                sp.wait_ge(w_split, 4 + p)
                load_w(0, p, (PIECES_AHEAD + p) % 2)
            for s in range(TURN):
                slot(0, s, False)
            with sp.Fori(1, TURNS - 1) as turn:
                for s in range(TURN):
                    slot(turn, s, False)
            for s in range(B + 2):
                slot(TURNS - 1, s, True)
            sp.wait_ge(w_stored, 16 * CHUNKS)
            sp.wait_ge(proj_done, nproj(TURNS - 1, latest(TILES, TURN, "k", 1)))

            def load_gu(j, i, free):
                if free:
                    sp.wait_ge(gu_split, j - 1)
                sp.dma_start(gu_raw[i][:, :], ff_w[:, bass.ds(j * FF_J, 2 * D)]).then_inc(gu_in[i], 16)

            def load_dn(j, i, free):
                if free:
                    sp.wait_ge(dn_split, j - 1)
                sp.dma_start(dn_raw[i][:, :], ff_w[:, bass.ds(j * FF_J + 2 * D, D)]).then_inc(dn_in[i], 16)

            for i in range(2):
                load_gu(i, i, False)
            for i in range(2):
                load_dn(i, i, False)
            with sp.Fori(1, MT // 2) as jj:
                for i in range(2):
                    load_gu(jj * 2 + i, i, True)
            with sp.Fori(1, MT // 2) as jj:
                for i in range(2):
                    load_dn(jj * 2 + i, i, True)
            for n, b in enumerate(DOWN_ORDER):
                sp.wait_ge(fin_done, n + 1)
                sp.dma_start(out[b], xs[:, b, :]).then_inc(out_done, 16)
            sp.wait_ge(out_done, 16 * B)

        @block.gpsimd
        def _(pool):
            def low_w(turn, p):
                pool.wait_ge(w_hi_done, npiece(turn, p))
                nc.gpsimd.tensor_tensor(piece(p, w_lo), piece_raw(p, (PIECES_AHEAD + p) % 2), f32(piece(p, w_hi)),
                                        ALU.subtract).then_inc(w_split, 1)

            def norm(n, i):
                pool.wait_ge(rinv_done, n + 1)
                nc.gpsimd.tensor_tensor(prob[i][:, :, :], prob[i][:, :, :], rinv[i][:, :].unsqueeze(2).to_broadcast([P, NE, P]),
                                        ALU.mult).then_inc(norm_done, 1)

            def scale(c, i, ahead):
                pool.wait_ge(qc_done, c + (1 + ahead))
                pool.wait_ge(absmax_in, (c + 1) * 32)
                wait_past(pool, w_stored, c * 16)
                pool.wait_ge(env_done, c + 1)
                nc.gpsimd.tensor_tensor(w_out[:, :], line[i][8, 9][:, :], absmax[:, :], ALU.mult).then_inc(w_scaled, 1)

            def chunk(c, i):
                if isinstance(c, int) and c < 2:
                    pool.wait_ge(qc_done, c + 1)
                else:
                    scale(c - 2, i, 2)
                for key in POOL_LINES:
                    a, o = LINE[key]
                    nc.gpsimd.tensor_scalar(line[i][key][:, :], q_c[i][:, :], a, o, ALU.mult, ALU.add).then_inc(pool_lines, 1)

            def slot(turn, s, last):
                n, b = before(turn, s, 0)
                if has_chunk(s, last):
                    chunk(n, b % 2)
                elif has_chunk(s - 2, last):
                    scale(turn * TURN + s - 2, b % 2, 0)
                if s < TURN:
                    norm(n, b % 2)
                for p in slot_pieces(s, last):
                    low_w(turn, p)
                if last and s - Y_LAG >= B:
                    ln_power(pool, LN_T, s - Y_LAG - B)

            def low_gu(j, i):
                pool.wait_ge(gu_hi_done, j + 1)
                nc.gpsimd.tensor_tensor(flat4(gu_lo[i]), gu_raw[i][:, :], f32(flat4(gu_hi[i])), ALU.subtract).then_inc(gu_split, 1)

            def low_dn(j, i):
                pool.wait_ge(dn_hi_done, j + 1)
                nc.gpsimd.tensor_tensor(dn_lo[i][:, :], dn_raw[i][:, :], f32(dn_hi[i][:, :]), ALU.subtract).then_inc(dn_split, 1)

            nc.gpsimd.memset(ident[:, :], 0.0).then_inc(ident_zero, 1)
            nc.gpsimd.memset(mask[:, :], 0.0).then_inc(mask_zero, 1)
            nc.gpsimd.memset(minus_half[:, :], -0.5).then_inc(half_set, 1)
            pool.wait_ge(ident_zero, 1)
            nc.gpsimd.affine_select(out=ident[:, :], in_=ident[:, :], compare_op=ALU.not_equal, fill=1.0, base=0,
                                    pattern=[[-1, P]], channel_multiplier=1).then_inc(ident_done, 1)
            pool.wait_ge(mask_zero, 1)
            nc.gpsimd.affine_select(out=mask[:, :], in_=mask[:, :], compare_op=ALU.is_ge, fill=MASKED, base=0,
                                    pattern=[[-1, P]], channel_multiplier=1).then_inc(mask_done, 1)
            pool.wait_ge(half_set, 1)
            for b in range(4):
                ln_power(pool, 0, b)
            for k in range(0, KT, 2):
                pool.wait_ge(ctx_hi_done, k + 1)
                nc.gpsimd.tensor_tensor(ctx_lo[:, k, :], ctx_raw[:, k, :], f32(ctx_hi[:, k, :]), ALU.subtract).then_inc(ctx_split, 1)
            for b in range(4, B):
                ln_power(pool, 0, b)

            for s in range(TURN):
                slot(0, s, False)
            with pool.Fori(1, TURNS - 1) as turn:
                for s in range(TURN):
                    slot(turn, s, False)
            for s in range(TURN + Y_LAG):
                slot(TURNS - 1, s, True)
                if TURN - 2 <= s < TURN:
                    low_gu(s - TURN + 2, s - TURN + 2)

            with pool.Fori(1, MT // 2) as jj:
                for i in range(2):
                    low_gu(jj * 2 + i, i)
            with pool.Fori(0, MT // 2) as jj:
                for i in range(2):
                    low_dn(jj * 2 + i, i)

        @block.scalar
        def _(act):
            def high_part(p, i):
                nc.scalar.activation(piece(p, w_hi), piece_raw(p, i), ACT.Copy).then_inc(w_hi_done, 1)

            def high_w(turn, p):
                slot, name = PIECES[p]
                nth = PIECES_AHEAD + p
                act.wait_ge(w_in[nth % 2], turn * (len(PIECES) // 2 * 16) + (nth // 2 + 1) * 16)
                if name[0] == "d":
                    wait_past(act, y_done, turn * TURN + slot // B * B)
                else:
                    user = ("v", 3) if name[0] == "v" else (name, 3 if name[0] == "q" else 1)
                    wait_past(act, proj_done, nproj(turn, latest(TILES, slot + 1, *user)))
                high_part(p, nth % 2)

            def proj_high(done, n, bank):
                act.wait_ge(proj_done, done + 1)
                nc.scalar.activation(proj_dst(n, v_hi, k_hi, q_hi), bank[:, :], ACT.Copy).then_inc(proj_hi, 1)

            def exps(n, i):
                act.wait_ge(bias_done, n + 1)
                for e in range(NE):
                    ins = nc.scalar.activation(prob[i][:, e, :], prob[i][:, e, :], ACT.Exp, bias=bias[i][:, e:e + 1],
                                               scale=SCALE, accum_out=rsum[i][:, e:e + 1])
                ins.then_inc(exp_done, 1)

            def pt_high(n):
                act.wait_ge(t_done, n + 1)
                nc.scalar.activation(flat(pt_hi), t_ps[:, :], ACT.Copy).then_inc(pt_hi_done, 1)

            def ot_high(n):
                act.wait_ge(o_done, n + 1)
                nc.scalar.activation(flat(ot_hi), o_ps[:, :], ACT.Copy).then_inc(ot_hi_done, 1)

            def chunk(c, i):
                act.wait_ge(qc_done, c + 1)
                wait_past(act, w_scaled, c - 1)
                for key in ACT_LINES:
                    fn = ACT.Relu if key == (8, 9) else ACT.Identity
                    nc.scalar.activation(line[i][key][:, :], q_c[i][:, :], fn, bias=line_at[:, key[0]:key[0] + 1],
                                         scale=LINE[key][0]).then_inc(act_lines, 1)

            def slot(turn, s, last):
                for n in second_tile(turn, s, last):
                    proj_high(made(turn, n), n, proj_bank(n))
                if s < TURN:
                    n, b = before(turn, s, 0)
                    exps(n, b % 2)
                pieces = slot_pieces(s, last)
                for p in pieces:
                    if PIECES[p][1][0] == "d":
                        high_w(turn, p)
                for n in slot_tiles(s, last)[:1]:
                    proj_high(made(turn, n), n, proj_bank(n))
                n, _ = before(turn, s, O_LAG)
                if n is not None:
                    ot_high(n)
                n, _ = before(turn, s, T_LAG)
                if n is not None:
                    pt_high(n)
                if has_chunk(s, last):
                    chunk(turn * TURN + s, s % 2)
                for p in pieces:
                    if PIECES[p][1][0] != "d":
                        high_w(turn, p)
                if last and s - TURN_LAG >= B:
                    ln_high(act, LN_T, s - TURN_LAG - B)

            def first_piece(i):
                act.wait_ge(w_in[i % 2], (i // 2 + 1) * 16)
                high_part(FIRST_PIECES[i], i % 2)

            def first_tile(i):
                proj_high(i, FIRST_TILES[i], proj_ps[i % 2])

            act.wait_ge(gates_in, 16)
            nc.scalar.activation(gate[:, :], gate_raw[:, :], ACT.Tanh).then_inc(gate_done, 1)
            act.wait_ge(line_at_set, len(ACT_LINES))
            first_piece(0)
            for b in range(2):
                ln_high(act, 0, b)
            first_piece(1)
            for k in range(KT):
                act.wait_ge(ctx_in[k], 16)
                nc.scalar.activation(ctx_hi[:, k, :], ctx_raw[:, k, :], ACT.Copy).then_inc(ctx_hi_done, 1)
                if k == 1:
                    first_tile(0)
            first_piece(2)
            first_tile(1)
            for b in range(2, 4):
                ln_high(act, 0, b)
            for i in range(3, 5):
                first_piece(i)
            for i in range(2, PROJ_AHEAD):
                first_tile(i)
                for b in range(2 * i, 2 * i + 2):
                    ln_high(act, 0, b)

            for s in range(TURN):
                slot(0, s, False)
            with act.Fori(1, TURNS - 1) as turn:
                for s in range(TURN):
                    slot(turn, s, False)

            def high_gu(j, i, pair):
                act.wait_ge(gu_in[i], (pair + 1) * 16)
                wait_past(act, u_done, 2 * (j - 1))
                nc.scalar.activation(flat4(gu_hi[i]), gu_raw[i][:, :], ACT.Copy).then_inc(gu_hi_done, 1)

            for s in range(TURN + TURN_LAG):
                slot(TURNS - 1, s, True)
                if TURN - 2 <= s < TURN:
                    high_gu(s - TURN + 2, s - TURN + 2, 0)

            def silu_of(seq, i, t):
                act.wait_ge(g_done, seq + 1)
                wait_past(act, h_done, seq - 1)
                nc.scalar.activation(silu[seq_buffer(seq, t)][:, :], g_ps[i][t][:, :], ACT.Silu).then_inc(silu_done, 1)

            def down_parts(jj, i):
                j = jj * 2 + i
                act.wait_ge(dn_in[i], (jj + 1) * 16)
                wait_past(act, down_done, j - 1)
                nc.scalar.activation(dn_hi[i][:, :], dn_raw[i][:, :], ACT.Copy).then_inc(dn_hi_done, 1)
                if isinstance(jj, int):
                    act.wait_ge(h_done, 2 * j + 2)
                nc.scalar.activation(h_hi[i][:, :], h_cols(j), ACT.Copy).then_inc(hh_done, 1)

            for seq, (j, t) in enumerate(FIRST_HALVES):
                silu_of(seq, j, t)
            act.wait_ge(u_done, 3)
            with act.Fori(1, MT // 2) as jj:
                for i in range(2):
                    high_gu(jj * 2 + i, i, jj)
                for i in range(2):
                    for t in range(2):
                        silu_of(jj * 4 + (i * 2 + t), i, t)
            for i in range(2):
                down_parts(0, i)
            with act.Fori(1, MT // 2) as jj:
                for i in range(2):
                    down_parts(jj, i)

        @block.vector
        def _(dve):
            def proj_low(done, n, bank):
                dve.wait_ge(proj_hi, done + 1)
                nc.vector.tensor_tensor(proj_dst(n, v_lo, k_lo, q_lo), bank[:, :],
                                        f32(proj_dst(n, v_hi, k_hi, q_hi)), ALU.subtract).then_inc(proj_split, 1)

            def softmax(n, i):
                dve.wait_ge(s_done, n + 1)
                nc.vector.tensor_tensor(prob[i][:, :, :], s_ps[i][:, :].rearrange("p (e k) -> p e k", e=NE),
                                        mask[:, :].unsqueeze(1).to_broadcast([P, NE, P]), ALU.add).then_inc(s_masked, 1)
                dve.wait_ge(s_masked, n + 1)
                nc.vector.tensor_reduce(bias[i][:, :], prob[i][:, :, :], AX_X, ALU.max).then_inc(max_done, 1)
                dve.wait_ge(max_done, n + 1)
                nc.vector.tensor_scalar(bias[i][:, :], bias[i][:, :], -SCALE, None, ALU.mult).then_inc(bias_done, 1)

            def rinvs(n, i):
                dve.wait_ge(exp_done, n + 1)
                nc.vector.reciprocal(rinv[i][:, :], rsum[i][:, :]).then_inc(rinv_done, 1)

            def pt_low(n):
                dve.wait_ge(pt_hi_done, n + 1)
                nc.vector.tensor_tensor(flat(pt_lo), t_ps[:, :], f32(flat(pt_hi)), ALU.subtract).then_inc(pt_split, 1)

            def ot_low(n):
                dve.wait_ge(ot_hi_done, n + 1)
                nc.vector.tensor_tensor(flat(ot_lo), o_ps[:, :], f32(flat(ot_hi)), ALU.subtract).then_inc(ot_split, 1)

            def add_y(n, b):
                dve.wait_ge(y_done, n + 1)
                nc.vector.scalar_tensor_tensor(xs[:, b, :], y_ps[b % 2][:, :], gate[:, 0:1], xs[:, b, :],
                                               ALU.mult, ALU.add).then_inc(y_added, 1)

            def codes(c, i):
                dve.wait_ge(q_in, (c + 1) * 16)
                nc.vector.tensor_scalar(q_c[i][:, :], q_raw[:, :], -7.0, None, ALU.add).then_inc(qc_done, 1)

            def envelope(c, i, steps):
                up, low = line[i][8, 9], line[i][0, 1]
                for step in steps:
                    if step < 2:
                        dve.wait_ge(*((act_lines, (c + 1) * 4), (pool_lines, (c + 1) * 3))[step])
                    else:
                        dve.wait_ge(env_step, c * 6 + (6 if step == 6 else step - 1))
                    if step in (0, 2, 4):
                        of = line[i][{0: (14, 15), 2: (10, 11), 4: (12, 13)}[step]]
                        nc.vector.tensor_tensor(up[:, :], up[:, :], of[:, :], ALU.max).then_inc(env_step, 1)
                    elif step in (1, 3):
                        of = line[i][{1: (2, 3), 3: (4, 5)}[step]]
                        nc.vector.tensor_tensor(low[:, :], low[:, :], of[:, :], ALU.min).then_inc(env_step, 1)
                    elif step == 5:
                        nc.vector.scalar_tensor_tensor(low[:, :], q_c[i][:, :], LINE[6, 7][0], low[:, :],
                                                       ALU.mult, ALU.min).then_inc(env_step, 1)
                    else:
                        nc.vector.scalar_tensor_tensor(up[:, :], low[:, :], 0.0, up[:, :], ALU.min, ALU.add).then_inc(env_done, 1)

            def residual(turn, s):
                n, b = before(turn, s, Y_LAG)
                if n is not None:
                    add_y(n, b)

            def second_ln(s, last):
                if last and B + Y_LAG <= s < TURN + Y_LAG:
                    ln_stats(dve, LN_T, s - Y_LAG - B)
                if last and B + Y_LAG + 1 <= s < TURN + Y_LAG + 1:
                    ln_norm(dve, LN_T, s - Y_LAG - 1 - B)

            def slot(turn, s, last):
                n, b = before(turn, s, 0)
                if s < TURN:
                    softmax(n, b % 2)
                for t in second_tile(turn, s, last):
                    proj_low(made(turn, t), t, proj_bank(t))
                chunk, i = before(turn, s, 1) if has_chunk(s - 1, last) else (None, 0)
                if chunk is not None:
                    envelope(chunk, i % 2, range(4))
                early = last and not slot_tiles(s, last)
                if early:
                    residual(turn, s)
                    if s < TURN:
                        second_ln(s, last)
                if s < TURN:
                    rinvs(n, b % 2)
                if chunk is not None:
                    envelope(chunk, i % 2, range(4, 5))
                for t in slot_tiles(s, last)[:1]:
                    proj_low(made(turn, t), t, proj_bank(t))
                if not early:
                    residual(turn, s)
                    second_ln(s, last)
                n, _ = before(turn, s, O_LAG)
                if n is not None:
                    ot_low(n)
                n, _ = before(turn, s, T_LAG)
                if n is not None:
                    pt_low(n)
                if s >= TURN:
                    second_ln(s, last)
                if chunk is not None:
                    envelope(chunk, i % 2, range(5, 7))
                if not last or has_chunk(s + 1, last):
                    codes(turn * TURN + (s + 1), (s + 1) % 2)
                if last and s - TURN_LAG >= B:
                    ln_low(dve, LN_T, s - TURN_LAG - B)

            def first_piece(i):
                dve.wait_ge(w_hi_done, i + 1)
                nc.vector.tensor_tensor(piece(FIRST_PIECES[i], w_lo), piece_raw(FIRST_PIECES[i], i % 2),
                                        f32(piece(FIRST_PIECES[i], w_hi)), ALU.subtract).then_inc(w_split, 1)

            def first_tile(i):
                proj_low(i, FIRST_TILES[i], proj_ps[i % 2])

            for key in ACT_LINES:
                nc.vector.memset(line_at[:, key[0]:key[0] + 1], LINE[key][1]).then_inc(line_at_set, 1)
            def pair(step, b):
                for n in (b, b + 1):
                    step(dve, 0, n)

            pair(ln_stats, 0)
            pair(ln_norm, 0)
            first_piece(0)
            pair(ln_low, 0)
            pair(ln_stats, 2)
            pair(ln_norm, 2)
            first_piece(1)
            for k in range(1, KT, 2):
                dve.wait_ge(ctx_hi_done, k + 1)
                nc.vector.tensor_tensor(ctx_lo[:, k, :], ctx_raw[:, k, :], f32(ctx_hi[:, k, :]), ALU.subtract).then_inc(ctx_split, 1)
                if k == 1:
                    first_tile(0)
            first_piece(2)
            first_tile(1)
            pair(ln_low, 2)
            pair(ln_stats, 4)
            pair(ln_norm, 4)
            for i in range(3, 5):
                first_piece(i)
            first_tile(2)
            pair(ln_low, 4)
            pair(ln_stats, 6)
            pair(ln_norm, 6)
            first_tile(3)
            pair(ln_low, 6)
            codes(0, 0)
            dve.wait_ge(gate_done, 1)
            dve.wait_ge(mask_done, 1)
            for s in range(TURN):
                slot(0, s, False)
            with dve.Fori(1, TURNS - 1) as turn:
                for s in range(TURN):
                    slot(turn, s, False)
            for s in range(TURN + TURN_LAG):
                slot(TURNS - 1, s, True)
            dve.wait_ge(w_stored, 16 * CHUNKS)

            def hidden_of(seq, j, i, t):
                dve.wait_ge(silu_done, seq + 1)
                dve.wait_ge(u_done, seq + 1)
                nc.vector.tensor_tensor(h_cols(j, t), u_ps[i][t][:, :], silu[seq_buffer(seq, t)][:, :], ALU.mult).then_inc(h_done, 1)

            def h_low(j, i):
                dve.wait_ge(hh_done, j + 1)
                nc.vector.tensor_tensor(h_lo[i][:, :], h_cols(j), f32(h_hi[i][:, :]), ALU.subtract).then_inc(h_split, 1)

            for seq, (j, t) in enumerate(FIRST_HALVES):
                hidden_of(seq, j, j, t)
            with dve.Fori(1, MT // 2 - 1) as jj:
                for i in range(2):
                    for t in range(2):
                        hidden_of(jj * 4 + (i * 2 + t), jj * 2 + i, i, t)
            for t in range(2):
                hidden_of(2 * MT - 4 + t, MT - 2, 0, t)
            dve.wait_ge(h_done, 2 * MT - 2)
            h_low(0, 0)
            for t in range(2):
                hidden_of(2 * MT - 2 + t, MT - 1, 1, t)
            dve.wait_ge(h_done, 2 * MT)
            h_low(1, 1)
            with dve.Fori(1, MT // 2) as jj:
                for i in range(2):
                    h_low(jj * 2 + i, i)
            for n, b in enumerate(DOWN_ORDER):
                dve.wait_ge(fin_ready, n + 1)
                nc.vector.scalar_tensor_tensor(xs[:, b, :], banks[b][:, :], gate[:, 1:2], xs[:, b, :],
                                               ALU.mult, ALU.add).then_inc(fin_done, 1)

        @block.tensor
        def _(pe):
            def product(dst, terms):
                for i, (a_hi, a_lo, b_hi, b_lo) in enumerate(terms):
                    nc.tensor.matmul(dst, a_hi, b_lo, start=(i == 0), stop=False)
                    nc.tensor.matmul(dst, a_lo, b_hi, start=False, stop=False)
                    mm = nc.tensor.matmul(dst, a_hi, b_hi, start=False, stop=(i == len(terms) - 1))
                return mm

            def project(done, n, dst):
                wait_past(pe, proj_split, done - 1)
                _, name, at = TILES[n]
                if name == "v":
                    for t in range(2):
                        toks = slice((at * 2 + t) * P, (at * 2 + t + 1) * P)
                        mm = product(dst[:, t * PAIR:(t + 1) * PAIR],
                                     [(ctx_hi[:, k, toks], ctx_lo[:, k, toks], wv(w_hi, k), wv(w_lo, k)) for k in range(KT)])
                elif name == "k":
                    cols = slice(at * HALF, (at + 1) * HALF)
                    mm = product(dst[:, :], [(wk(w_hi, k), wk(w_lo, k), ctx_hi[:, k, cols], ctx_lo[:, k, cols]) for k in range(KT)])
                else:
                    cols = slice(at * PAIR, (at + 1) * PAIR)
                    for t in range(2):
                        e = int(name[1]) * 2 + t
                        mm = product(dst[:, t * PAIR:(t + 1) * PAIR],
                                     [(wq(w_hi, k, e), wq(w_lo, k, e), ln_hi[:, k, cols], ln_lo[:, k, cols]) for k in range(KT)])
                mm.then_inc(proj_done, 1)

            def scores(n, b):
                wait_past(pe, s_masked, n - 1)
                at = slice(b % 2 * P, (b % 2 + 1) * P)
                keys = slice(b * P, (b + 1) * P)
                for e in range(NE):
                    mm = product(s_ps[b % 2][:, e * P:(e + 1) * P],
                                 [(q_hi[:, b // 2 % 2, e, at], q_lo[:, b // 2 % 2, e, at], k_hi[:, keys], k_lo[:, keys])])
                mm.then_inc(s_done, 1)

            def turn_over(n, i):
                pe.wait_ge(norm_done, n + 1)
                wait_past(pe, pt_split, n)
                for e in range(NE):
                    mm = nc.tensor.transpose(t_ps[:, e * P:(e + 1) * P], prob[i][:, e, :], ident[:, :])
                mm.then_inc(t_done, 1)

            def attend(n, b, of):
                pe.wait_ge(pt_split, n + 1)
                wait_past(pe, ot_split, n)
                product(o_ps[:, :], [(v_hi[:, b, of, :], v_lo[:, b, of, :], flat(pt_hi), flat(pt_lo))]).then_inc(o_done, 1)

            def out_project(n, b, half_of_wd):
                pe.wait_ge(ot_split, n + 1)
                wait_past(pe, y_added, n - 1)
                for e in range(NE):
                    if b == 0 and e % 2 == 0:
                        pe.wait_ge(w_split, half_of_wd[e // 2])
                    nc.tensor.matmul(y_ps[b % 2][:, :], ot_hi[:, e, :], wd(w_lo, e), start=(e == 0), stop=False)
                    nc.tensor.matmul(y_ps[b % 2][:, :], ot_lo[:, e, :], wd(w_hi, e), start=False, stop=False)
                    mm = nc.tensor.matmul(y_ps[b % 2][:, :], ot_hi[:, e, :], wd(w_hi, e), start=False, stop=(e == NE - 1))
                mm.then_inc(y_done, 1)

            def hidden_tile(i, a, t):
                cols = slice(t * HALF, (t + 1) * HALF)
                product((g_ps, u_ps)[a][i][t][:, :], [(gu_hi[i][:, a, k, :], gu_lo[i][:, a, k, :], ln_hi[:, k, cols], ln_lo[:, k, cols])
                                                      for k in range(KT)]).then_inc((g_done, u_done)[a], 1)

            def tiles(turn, numbers, s):
                for t in numbers:
                    _, name, at = TILES[t]
                    if at == 0:
                        pe.wait_ge(w_split, npiece(turn, latest(PIECES, s, "v1" if name == "v" else name)))
                    project(made(turn, t), t, proj_bank(t))

            def slot(turn, s, last):
                if s < TURN:
                    n, b = before(turn, s, 0)
                    if b % 2 == 0:
                        pe.wait_ge(proj_split, nproj(turn, latest(TILES, s, "q1", b // 2)))
                    scores(n, b)
                if isinstance(turn, int) and turn == 0 and s == 2:
                    pe.wait_ge(ln_split, B)
                n, b = before(turn, s, Y_LAG)
                if b != B - 1:
                    tiles(turn, slot_tiles(s, last)[:1], s)
                if n is not None:
                    out_project(n, b, [npiece(turn, latest(PIECES, s, name)) for name in ("d0", "d1")])
                if b == B - 1:
                    tiles(turn, slot_tiles(s, last)[:1], s)
                n, b = before(turn, s, O_LAG)
                if n is not None:
                    if O_LAG <= s < B + O_LAG and b % 2 == 0:
                        pe.wait_ge(proj_split, nproj(turn, latest(TILES, s, "v", b // 2)))
                    attend(n, b, (s - O_LAG) // B % 2)
                n, b = before(turn, s, T_LAG)
                if n is not None:
                    turn_over(n, b % 2)
                tiles(turn, slot_tiles(s, last)[1:], s)
                if last and s == B + TURN_LAG:
                    pe.wait_ge(proj_split, nproj(turn, latest(TILES, s, "q0", 3)))
                if last and 0 <= s - TURN_LAG - B < 6:
                    ln_turn(pe, LN_T, s - TURN_LAG - B)
                if last and s == TURN + O_LAG - 1:
                    pe.wait_ge(gu_split, 1)
                    pe.wait_ge(ln_split, LN_T + B // 2)
                    hidden_tile(0, 0, 0)
                if last and s == TURN + Y_LAG - 1:
                    hidden_tile(0, 1, 0)

            pe.wait_ge(ident_done, 1)
            for b in range(2):
                ln_turn(pe, 0, b)
            pe.wait_ge(ln_split, 2)
            for i in range(PROJ_AHEAD):
                if i == 2:
                    pe.wait_ge(ctx_split, KT)
                pe.wait_ge(w_split, i + 1 if i < 3 else 5)
                project(i, FIRST_TILES[i], proj_ps[i % 2])
                if i:
                    for b in range(2 * i, 2 * i + 2):
                        ln_turn(pe, 0, b)
            pe.wait_ge(ln_split, 4)
            for s in range(TURN):
                slot(0, s, False)
            with pe.Fori(1, TURNS - 1) as turn:
                for s in range(TURN):
                    slot(turn, s, False)
            for s in range(TURN + Y_LAG):
                slot(TURNS - 1, s, True)

            def hidden(j, i):
                pe.wait_ge(gu_split, j + 1)
                wait_past(pe, h_done, 2 * (j - 1))
                for a in range(2):
                    for t in range(2):
                        hidden_tile(i, a, t)

            ln_turn(pe, LN_T, 6)
            pe.wait_ge(gu_split, 2)
            hidden_tile(1, 0, 0)
            ln_turn(pe, LN_T, 7)
            pe.wait_ge(ln_split, LN_T + 7)
            hidden_tile(1, 1, 0)
            pe.wait_ge(ln_split, LN_T + B)
            for j in range(2):
                for a in range(2):
                    hidden_tile(j, a, 1)
            pe.wait_ge(h_done, 3)
            with pe.Fori(1, MT // 2) as jj:
                for i in range(2):
                    hidden(jj * 2 + i, i)
            pe.wait_ge(h_done, 2 * MT - 2)

            def down(jj, first, last):
                for i in range(2):
                    j = jj * 2 + i
                    pe.wait_ge(dn_split, j + 1)
                    pe.wait_ge(h_split, j + 1)
                    for n, b in enumerate(DOWN_ORDER):
                        if first and i == 0 and n == B // 2:
                            pe.wait_ge(h_done, 2 * MT)
                        toks = slice(b * P, (b + 1) * P)
                        nc.tensor.matmul(banks[b][:, :], h_hi[i][:, toks], dn_lo[i][:, :], start=(first and i == 0), stop=False)
                        nc.tensor.matmul(banks[b][:, :], h_lo[i][:, toks], dn_hi[i][:, :], start=False, stop=False)
                        mm = nc.tensor.matmul(banks[b][:, :], h_hi[i][:, toks], dn_hi[i][:, :], start=False, stop=(last and i == 1))
                        if last and i == 1:
                            mm.then_inc(fin_ready, 1)
                    if not (last and i == 1):
                        mm.then_inc(down_done, 1)

            down(0, True, False)
            with pe.Fori(1, MT // 2 - 1) as jj:
                down(jj, False, False)
            down(MT // 2 - 1, False, True)


_INS = ['x', 'ctx_4096', 'g_xattn', 'g_ffn', 'L0_xattn_Wq', 'L0_xattn_Wk', 'L0_xattn_Wv', 'L0_xattn_Wd',
        'L0_ffn_gate_q', 'L0_ffn_gate_absmax', 'L0_ffn_up_q', 'L0_ffn_up_absmax', 'L0_ffn_down_q', 'L0_ffn_down_absmax']


def lay_out(x, ctx_4096, g_xattn, g_ffn, L0_xattn_Wq, L0_xattn_Wk, L0_xattn_Wv, L0_xattn_Wd,
            L0_ffn_gate_q, L0_ffn_gate_absmax, L0_ffn_up_q, L0_ffn_up_absmax, L0_ffn_down_q, L0_ffn_down_absmax):
    import numpy as np
    wk = L0_xattn_Wk.reshape(NG, P, KT, P).transpose(0, 3, 2, 1).reshape(NG, P, KT * P)
    wv = L0_xattn_Wv.reshape(NG // 2, 2 * P, KT, P).transpose(0, 3, 2, 1).reshape(NG // 2, P, KT * 2 * P)
    wq = L0_xattn_Wq.reshape(NG, 2, 2 * P, KT, P).transpose(0, 4, 1, 3, 2).reshape(NG, P, KT * NE * P)
    wd = L0_xattn_Wd.reshape(D, NG, NE, P).transpose(1, 3, 2, 0).reshape(NG, P, NE * D)
    gu = [q.reshape(MT, P, KT, P).transpose(3, 0, 2, 1).reshape(P, MT, D) for q in (L0_ffn_gate_q, L0_ffn_up_q)]
    down = L0_ffn_down_q.reshape(D, MT, P).transpose(2, 1, 0)
    gu_absmax = [a.reshape(MT, P, KT, 2).transpose(3, 0, 2, 1).reshape(2, MT, D) for a in (L0_ffn_gate_absmax, L0_ffn_up_absmax)]
    down_absmax = L0_ffn_down_absmax.reshape(D, MT, 2).transpose(2, 1, 0)
    return {
        "x": x,
        "ctx_t": ctx_4096.reshape(TOK, D).T,
        "gates": np.concatenate([g_xattn, g_ffn]),
        "w_groups": np.concatenate([wq, wk, wd], axis=2).transpose(1, 0, 2).reshape(P, NG * W_G),
        "w_v": wv.transpose(1, 0, 2).reshape(P, NG // 2 * W_V),
        "ff_q": np.concatenate([*gu, down], axis=2).reshape(P, FF),
        "ff_absmax": np.concatenate([*gu_absmax, down_absmax], axis=2).reshape(2, FF),
    }


def kernel(**inputs):
    import numpy as _np
    import concourse.bacc as _bacc
    from concourse.bass_utils import run_bass_kernel_spmd as _run

    nc = _bacc.Bacc("TRN2", target_bir_lowering=False, num_devices=1, dynamic_dma_scratch_size=1024)
    laid = {k: _np.ascontiguousarray(v) for k, v in lay_out(**{n: _np.asarray(inputs[n]) for n in _INS}).items()}
    args = {k: nc.dram_tensor(f"in_{k}", v.shape, mybir.dt.from_np(v.dtype), kind="ExternalInput").ap() for k, v in laid.items()}
    out = nc.dram_tensor("out_0_dram", (B, S, D), F32, kind="ExternalOutput").ap()
    flamingo(nc, **args, out=out)
    r = _run(nc, [{f"in_{k}": v for k, v in laid.items()}], core_ids=[0])
    return r.results[0]["out_0_dram"]
```
